# Optimizing a Trainium2 kernel written in Bass

```python
import numpy as np
import jax
import jax.numpy as jnp

def _softmax(x, axis=-1):
    return jax.nn.softmax(x, axis=axis)

def _gelu(x):
    return jax.nn.gelu(x, approximate=True)

def _silu(x):
    return jax.nn.silu(x)

def _sigmoid(x):
    return jax.nn.sigmoid(x)

def _layernorm(x, axis=-1, eps=1e-05):
    m = jnp.mean(x, axis=axis, keepdims=True)
    v = jnp.var(x, axis=axis, keepdims=True)
    return (x - m) / jnp.sqrt(v + eps)

def _scatter_add(tgt, idx, src, axis=0):
    return tgt.at[idx].add(src)

def _segment_sum(src, seg, n):
    return jax.ops.segment_sum(src, seg, n)
kernel_name = 'mk_decoder_preln_d1_seqx_r8_3d35d0'

def setup_inputs(seed: int=0):
    np.random.seed(seed)
    _w = jnp.asarray

    def _rec_inputs():
        import jax
        import jax.numpy as jnp
        _rk = jax.random.key(seed)
        x = -0.0002928 + 1 * jax.random.normal(jax.random.fold_in(_rk, 1), (64, 128, 128), jnp.float32)
        _lenS = 128 - jax.random.randint(jax.random.fold_in(_rk, 7), (64,), 0, max(1, 128 // 4) + 1, jnp.int32)
        _lenS2 = 120 - jax.random.randint(jax.random.fold_in(_rk, 8), (64,), 0, max(1, 120 // 4) + 1, jnp.int32)
        _ctx_1024P = jax.random.normal(jax.random.fold_in(_rk, 11), (64, 16, 128), jnp.float32)
        _ctx_1024c = jax.random.dirichlet(jax.random.fold_in(_rk, 511), 0.3 * jnp.ones((16,), jnp.float32), (64, 120))
        _ctx_1024t = jnp.einsum('bsk,bkd->bsd', _ctx_1024c, _ctx_1024P)
        _ctx_1024t = _ctx_1024t * jax.lax.rsqrt(jnp.mean(jnp.square(_ctx_1024t)) + 1e-12) * 0.953939
        ctx_1024 = -1.39393e-06 + 0.999914 * (_ctx_1024t + 0.3 * jax.random.normal(jax.random.fold_in(_rk, 611), (64, 120, 128), jnp.float32))
        _validS = jnp.arange(128)[None, :] < _lenS[:, None]
        _validS2 = jnp.arange(120)[None, :] < _lenS2[:, None]
        _causal = jnp.tril(jnp.ones((128, 128), dtype=bool))
        mask_Bx1xS2x1_bk0 = jnp.logical_not(jnp.ones((64, 1, 120, 1), dtype=bool))
        return (x, ctx_1024, mask_Bx1xS2x1_bk0)
    x, ctx_1024, mask_Bx1xS2x1_bk0 = _rec_inputs()

    def _L0_attn_setup():
        import jax, jax.numpy as jnp
        import numpy as np
        D_MODEL, N_HEADS = (128, 16)
        D_H = D_MODEL // N_HEADS
        D_HR = D_H // 2
        D_LATENT = 32
        THETA = 10000.0

        def rope(x, theta=THETA):
            S, d = (x.shape[-2], x.shape[-1])
            inv = theta ** (-jnp.arange(0, d, 2, dtype=jnp.float32) / d)
            ang = jnp.arange(S, dtype=jnp.float32)[:, None] * inv
            cos, sin = (jnp.cos(ang), jnp.sin(ang))
            x1, x2 = (x[..., 0::2], x[..., 1::2])
            r1 = x1 * cos - x2 * sin
            r2 = x1 * sin + x2 * cos
            return jnp.stack([r1, r2], axis=-1).reshape(x.shape)
        key = jax.random.key(seed)
        ks = jax.random.split(key, 9)
        s = lambda fan_in: 1.0 / np.sqrt(fan_in)
        return {'x': jax.random.normal(ks[0], (4, 256, D_MODEL), jnp.float32), 'W_DQ': jax.random.normal(ks[1], (D_MODEL, D_LATENT), jnp.float32) * s(D_MODEL), 'W_UQ': jax.random.normal(ks[2], (D_LATENT, N_HEADS * D_H), jnp.float32) * s(D_LATENT), 'W_QR': jax.random.normal(ks[3], (D_LATENT, N_HEADS * D_HR), jnp.float32) * s(D_LATENT), 'W_DKV': jax.random.normal(ks[4], (D_MODEL, D_LATENT), jnp.float32) * s(D_MODEL), 'W_UK': jax.random.normal(ks[5], (D_LATENT, N_HEADS * D_H), jnp.float32) * s(D_LATENT), 'W_UV': jax.random.normal(ks[6], (D_LATENT, N_HEADS * D_H), jnp.float32) * s(D_LATENT), 'W_KR': jax.random.normal(ks[7], (D_MODEL, D_HR), jnp.float32) * s(D_MODEL), 'W_O': jax.random.normal(ks[8], (N_HEADS * D_H, D_MODEL), jnp.float32) * s(N_HEADS * D_H)}
    _L0_attn_all = _L0_attn_setup()
    _L0_attn_in = {k: v for k, v in _L0_attn_all.items() if k in ('W_DQ', 'W_UQ', 'W_QR', 'W_DKV', 'W_UK', 'W_UV', 'W_KR', 'W_O')}
    del _L0_attn_all

    def _L0_xattn_setup():
        import jax, jax.numpy as jnp
        import numpy as np
        import math
        D_MODEL = 128
        N_HEADS = 16
        HEAD_DIM = D_MODEL // N_HEADS
        MLP_DIM = 4 * D_MODEL
        B, L, M = (2, 256, 256)

        def layer_norm(x, g, b, eps=1e-05):
            mu = jnp.mean(x, axis=-1, keepdims=True)
            var = jnp.var(x, axis=-1, keepdims=True)
            return (x - mu) * jax.lax.rsqrt(var + eps) * g + b

        def mha(q_in, k_in, qW, wW, oW, mask=None):
            b, l, _ = q_in.shape
            m = k_in.shape[1]
            q = (q_in @ qW).reshape(b, l, HEAD_DIM, N_HEADS)
            k = (k_in @ wW).reshape(b, m, HEAD_DIM, N_HEADS)
            s = jnp.einsum('bldn,bmdn->blmn', q, k)
            if mask is not None:
                s = jnp.where(mask, -1000000000.0, s)
            s = s / math.sqrt(HEAD_DIM)
            w = jax.nn.softmax(s, axis=2)
            x = jnp.einsum('blmn,bmdn->bldn', w, k)
            x = x.reshape(b, l, HEAD_DIM * N_HEADS)
            return x @ oW
        key = jax.random.key(seed)
        ks = jax.random.split(key, 16)
        sc = 1.0 / math.sqrt(D_MODEL)
        inp = {'x': jax.random.normal(ks[0], (B, L, D_MODEL), jnp.float32), 'enc_output': jax.random.normal(ks[1], (B, M, D_MODEL), jnp.float32), 'mask': jax.random.randint(ks[2], (B, 1, M, 1), 0, 2).astype(bool), 'q1W': jax.random.normal(ks[3], (D_MODEL, D_MODEL), jnp.float32) * sc, 'w1W': jax.random.normal(ks[4], (D_MODEL, D_MODEL), jnp.float32) * sc, 'o1W': jax.random.normal(ks[5], (D_MODEL, D_MODEL), jnp.float32) * sc, 'q2W': jax.random.normal(ks[6], (D_MODEL, D_MODEL), jnp.float32) * sc, 'w2W': jax.random.normal(ks[7], (D_MODEL, D_MODEL), jnp.float32) * sc, 'o2W': jax.random.normal(ks[8], (D_MODEL, D_MODEL), jnp.float32) * sc, 'ffW1': jax.random.normal(ks[9], (D_MODEL, MLP_DIM), jnp.float32) * sc, 'ffb1': jnp.zeros((MLP_DIM,), jnp.float32), 'ffW2': jax.random.normal(ks[10], (MLP_DIM, D_MODEL), jnp.float32) * sc, 'ffb2': jnp.zeros((D_MODEL,), jnp.float32), 'g1': jnp.ones((D_MODEL,), jnp.float32), 'b1': jnp.zeros((D_MODEL,), jnp.float32), 'g2': jnp.ones((D_MODEL,), jnp.float32), 'b2': jnp.zeros((D_MODEL,), jnp.float32), 'g3': jnp.ones((D_MODEL,), jnp.float32), 'b3': jnp.zeros((D_MODEL,), jnp.float32)}
        return inp
    _L0_xattn_all = _L0_xattn_setup()
    _L0_xattn_in = {k: v for k, v in _L0_xattn_all.items() if k in ('q1W', 'w1W', 'o1W', 'q2W', 'w2W', 'o2W', 'ffW1', 'ffb1', 'ffW2', 'ffb2', 'g1', 'b1', 'g2', 'b2', 'g3', 'b3')}
    del _L0_xattn_all

    def _L0_ffn_setup():
        import jax, jax.numpy as jnp
        import numpy as np
        HIDDEN = 128
        NUM_EXPERTS = 16
        TOP_K = 6
        EPS = 1e-10
        key = jax.random.key(seed)
        k1, k2, k3, k4 = jax.random.split(key, 4)
        tokens = jax.random.normal(k1, (4, 256, HIDDEN), dtype=jnp.float32)
        bound = 1.0 / np.sqrt(HIDDEN)
        router_w = jax.random.uniform(k2, (NUM_EXPERTS, HIDDEN), jnp.float32, -bound, bound)
        router_b = jax.random.uniform(k3, (NUM_EXPERTS,), jnp.float32, -bound, bound)
        expert_w = jax.random.normal(k4, (NUM_EXPERTS, HIDDEN, HIDDEN), dtype=jnp.float32) / np.sqrt(HIDDEN)
        return {'tokens': tokens, 'router_w': router_w, 'router_b': router_b, 'expert_w': expert_w}
    _L0_ffn_all = _L0_ffn_setup()
    _L0_ffn_in = {k: v for k, v in _L0_ffn_all.items() if k in ('router_w', 'router_b', 'expert_w')}
    del _L0_ffn_all
    return {'x': x, 'ctx_1024': ctx_1024, 'mask_Bx1xS2x1_bk0': mask_Bx1xS2x1_bk0, 'L0_attn_W_DQ': _L0_attn_in['W_DQ'], 'L0_attn_W_UQ': _L0_attn_in['W_UQ'], 'L0_attn_W_QR': _L0_attn_in['W_QR'], 'L0_attn_W_DKV': _L0_attn_in['W_DKV'], 'L0_attn_W_UK': _L0_attn_in['W_UK'], 'L0_attn_W_UV': _L0_attn_in['W_UV'], 'L0_attn_W_KR': _L0_attn_in['W_KR'], 'L0_attn_W_O': _L0_attn_in['W_O'], 'L0_xattn_q1W': _L0_xattn_in['q1W'], 'L0_xattn_w1W': _L0_xattn_in['w1W'], 'L0_xattn_o1W': _L0_xattn_in['o1W'], 'L0_xattn_q2W': _L0_xattn_in['q2W'], 'L0_xattn_w2W': _L0_xattn_in['w2W'], 'L0_xattn_o2W': _L0_xattn_in['o2W'], 'L0_xattn_ffW1': _L0_xattn_in['ffW1'], 'L0_xattn_ffb1': _L0_xattn_in['ffb1'], 'L0_xattn_ffW2': _L0_xattn_in['ffW2'], 'L0_xattn_ffb2': _L0_xattn_in['ffb2'], 'L0_xattn_g1': _L0_xattn_in['g1'], 'L0_xattn_b1': _L0_xattn_in['b1'], 'L0_xattn_g2': _L0_xattn_in['g2'], 'L0_xattn_b2': _L0_xattn_in['b2'], 'L0_xattn_g3': _L0_xattn_in['g3'], 'L0_xattn_b3': _L0_xattn_in['b3'], 'L0_ffn_router_w': _L0_ffn_in['router_w'], 'L0_ffn_router_b': _L0_ffn_in['router_b'], 'L0_ffn_expert_w': _L0_ffn_in['expert_w']}

def reference(x, ctx_1024, mask_Bx1xS2x1_bk0, L0_attn_W_DQ, L0_attn_W_UQ, L0_attn_W_QR, L0_attn_W_DKV, L0_attn_W_UK, L0_attn_W_UV, L0_attn_W_KR, L0_attn_W_O, L0_xattn_q1W, L0_xattn_w1W, L0_xattn_o1W, L0_xattn_q2W, L0_xattn_w2W, L0_xattn_o2W, L0_xattn_ffW1, L0_xattn_ffb1, L0_xattn_ffW2, L0_xattn_ffb2, L0_xattn_g1, L0_xattn_b1, L0_xattn_g2, L0_xattn_b2, L0_xattn_g3, L0_xattn_b3, L0_ffn_router_w, L0_ffn_router_b, L0_ffn_expert_w):
    import jax
    import jax.numpy as jnp

    def _L0_attn_ref(x, W_DQ, W_UQ, W_QR, W_DKV, W_UK, W_UV, W_KR, W_O):
        import jax, jax.numpy as jnp
        import numpy as np
        D_MODEL, N_HEADS = (128, 16)
        D_H = D_MODEL // N_HEADS
        D_HR = D_H // 2
        D_LATENT = 32
        THETA = 10000.0

        def rope(x, theta=THETA):
            S, d = (x.shape[-2], x.shape[-1])
            inv = theta ** (-jnp.arange(0, d, 2, dtype=jnp.float32) / d)
            ang = jnp.arange(S, dtype=jnp.float32)[:, None] * inv
            cos, sin = (jnp.cos(ang), jnp.sin(ang))
            x1, x2 = (x[..., 0::2], x[..., 1::2])
            r1 = x1 * cos - x2 * sin
            r2 = x1 * sin + x2 * cos
            return jnp.stack([r1, r2], axis=-1).reshape(x.shape)
        B, S, _ = x.shape
        d_qk = D_H + D_HR
        c_q = x @ W_DQ
        Qc = (c_q @ W_UQ).reshape(B, S, N_HEADS, D_H).transpose(0, 2, 1, 3)
        Qr = (c_q @ W_QR).reshape(B, S, N_HEADS, D_HR).transpose(0, 2, 1, 3)
        Qr = rope(Qr)
        c_kv = x @ W_DKV
        Kc = (c_kv @ W_UK).reshape(B, S, N_HEADS, D_H).transpose(0, 2, 1, 3)
        Kr = rope((x @ W_KR)[:, None, :, :])
        Kr = jnp.broadcast_to(Kr, (B, N_HEADS, S, D_HR))
        V = (c_kv @ W_UV).reshape(B, S, N_HEADS, D_H).transpose(0, 2, 1, 3)
        Q = jnp.concatenate([Qc, Qr], axis=-1)
        K = jnp.concatenate([Kc, Kr], axis=-1)
        scores = jnp.einsum('bhqd,bhkd->bhqk', Q, K)
        scores = jnp.clip(scores, -80.0, 80.0)
        causal = jnp.tril(jnp.ones((S, S), dtype=bool))
        scores = jnp.where(causal, scores, -jnp.inf)
        weights = jax.nn.softmax(scores / jnp.sqrt(jnp.float32(d_qk)), axis=-1)
        attn = jnp.einsum('bhqk,bhkd->bhqd', weights, V)
        attn = attn.transpose(0, 2, 1, 3).reshape(B, S, N_HEADS * D_H)
        return attn @ W_O

    def _L0_xattn_ref(x, enc_output, mask, q1W, w1W, o1W, q2W, w2W, o2W, ffW1, ffb1, ffW2, ffb2, g1, b1, g2, b2, g3, b3):
        import jax, jax.numpy as jnp
        import numpy as np
        import math
        D_MODEL = 128
        N_HEADS = 16
        HEAD_DIM = D_MODEL // N_HEADS
        MLP_DIM = 4 * D_MODEL
        B, L, M = (2, 256, 256)

        def layer_norm(x, g, b, eps=1e-05):
            mu = jnp.mean(x, axis=-1, keepdims=True)
            var = jnp.var(x, axis=-1, keepdims=True)
            return (x - mu) * jax.lax.rsqrt(var + eps) * g + b

        def mha(q_in, k_in, qW, wW, oW, mask=None):
            b, l, _ = q_in.shape
            m = k_in.shape[1]
            q = (q_in @ qW).reshape(b, l, HEAD_DIM, N_HEADS)
            k = (k_in @ wW).reshape(b, m, HEAD_DIM, N_HEADS)
            s = jnp.einsum('bldn,bmdn->blmn', q, k)
            if mask is not None:
                s = jnp.where(mask, -1000000000.0, s)
            s = s / math.sqrt(HEAD_DIM)
            w = jax.nn.softmax(s, axis=2)
            x = jnp.einsum('blmn,bmdn->bldn', w, k)
            x = x.reshape(b, l, HEAD_DIM * N_HEADS)
            return x @ oW
        sa = mha(x, x, q1W, w1W, o1W, mask=None)
        x = layer_norm(x + sa, g1, b1)
        ca = mha(x, enc_output, q2W, w2W, o2W, mask=mask)
        x = layer_norm(x + ca, g2, b2)
        h = jax.nn.gelu(x @ ffW1 + ffb1, approximate=False)
        ff = h @ ffW2 + ffb2
        x = layer_norm(x + ff, g3, b3)
        return x

    def _L0_ffn_ref(tokens, router_w, router_b, expert_w):
        import jax, jax.numpy as jnp
        import numpy as np
        HIDDEN = 128
        NUM_EXPERTS = 16
        TOP_K = 6
        EPS = 1e-10
        B, S, H = tokens.shape
        E = expert_w.shape[0]
        T = B * S
        logits = jnp.einsum('bsh,eh->bse', tokens, router_w) + router_b
        probs = jax.nn.softmax(logits, axis=-1)
        top_p, top_i = jax.lax.top_k(probs, TOP_K)
        top_p = top_p / (jnp.sum(top_p, axis=-1, keepdims=True) + EPS)
        x = tokens.reshape(T, H)
        flat_i = top_i.reshape(T, TOP_K)
        flat_p = top_p.reshape(T, TOP_K)
        gate = jnp.zeros((T, E), dtype=flat_p.dtype)
        gate = gate.at[jnp.arange(T)[:, None], flat_i].add(flat_p)
        acc = jnp.maximum(jnp.sum(gate, axis=-1), EPS)
        out = jnp.zeros_like(x)
        for e in range(E):
            out = out + x @ expert_w[e] * gate[:, e:e + 1]
        out = (out / acc[:, None]).reshape(B, S, H)
        out = out + EPS * jnp.sum(top_p, axis=-1, keepdims=True)
        return out
    x = x + _L0_attn_ref(_layernorm(x, axis=-1), L0_attn_W_DQ, L0_attn_W_UQ, L0_attn_W_QR, L0_attn_W_DKV, L0_attn_W_UK, L0_attn_W_UV, L0_attn_W_KR, L0_attn_W_O)
    x = x + _L0_xattn_ref(_layernorm(x, axis=-1), ctx_1024, mask_Bx1xS2x1_bk0, L0_xattn_q1W, L0_xattn_w1W, L0_xattn_o1W, L0_xattn_q2W, L0_xattn_w2W, L0_xattn_o2W, L0_xattn_ffW1, L0_xattn_ffb1, L0_xattn_ffW2, L0_xattn_ffb2, L0_xattn_g1, L0_xattn_b1, L0_xattn_g2, L0_xattn_b2, L0_xattn_g3, L0_xattn_b3)
    x = x + _L0_ffn_ref(_layernorm(x, axis=-1), L0_ffn_router_w, L0_ffn_router_b, L0_ffn_expert_w)
    return x

_drawn_inputs = setup_inputs


def setup_inputs(seed=0):
    import zlib

    import numpy as np

    out = dict(_drawn_inputs(seed))
    spreads = {'L0_xattn_ffb1': (0.0, 0.1),
     'L0_xattn_ffb2': (0.0, 0.1),
     'L0_xattn_g1': (1.0, 0.2),
     'L0_xattn_b1': (0.0, 0.1),
     'L0_xattn_g2': (1.0, 0.2),
     'L0_xattn_b2': (0.0, 0.1),
     'L0_xattn_g3': (1.0, 0.2),
     'L0_xattn_b3': (0.0, 0.1)}
    factors = {}
    for name, (base, spread) in spreads.items():
        noise = np.random.default_rng([zlib.crc32(name.encode()), seed]).standard_normal(out[name].shape)
        drawn = base * np.exp(spread * noise) if base else spread * noise
        out[name] = jnp.asarray(drawn.astype(out[name].dtype))
    for name, factor in factors.items():
        out[name] = (out[name] * factor).astype(out[name].dtype)
    return out
```

```python
import math
from contextlib import ExitStack

import numpy as np
import concourse.bass as bass
from concourse import mybir

F32 = mybir.dt.float32
F16 = mybir.dt.float16
BF16 = mybir.dt.bfloat16
U8 = mybir.dt.uint8
ALU = mybir.AluOpType
ACT = mybir.ActivationFunctionType
AX = mybir.AxisListType.X

B, S, D = 64, 128, 128
SC = 120
H, DH, DR, DL = 16, 8, 4, 32
FF = 4 * D
E, TOPK = 16, 6
NJ, NG = 4, H // 4
QW = 4
NQ = B // QW
LN_EPS = 1e-5
MOE_EPS = 1e-10
CLIP = 80.0
MASKED = -998244352.0
SCALE_MLA = 1.0 / math.sqrt(DH + DR)
SCALE_X = 1.0 / math.sqrt(DH)
P_LO = math.exp(-CLIP * SCALE_MLA)
MQ, MK, MV, MR = 0, H * DH, 2 * H * DH, 3 * H * DH
MEND = MR + H * DR + DR
ROWS_MLA = 2 * (DH + DR)
MLA, SA, CA = 0, 1, 2


LEAD = 16


class Signal:

    def __init__(self, sem, base=0):
        self.sem, self.base = sem, LEAD + base

    def at(self, n):
        return self.base + n


def apart(eng):
    eng.nop(nofuse=True)


def decoder_kernel(nc, a, out):
    ctx = ExitStack()
    with ctx:
        def sb(name, shape, dt=F32):
            return ctx.enter_context(nc.sbuf_tensor(name, shape, dt))

        def ps(name, shape, dt=F32):
            return ctx.enter_context(nc.psum_tensor(name, shape, dt))

        def sem(name):
            return ctx.enter_context(nc.semaphore(name))

        X = sb("X", [128, B, D])
        Y = sb("Y", [128, B, D])
        T = sb("T", [128, B, 128])
        L = sb("L", [128, B, E])
        id32 = sb("id32", [128, 128])
        id16 = sb("id16", [128, 128], F16)
        idb = sb("idb", [128, 128], BF16)
        cosT = sb("cosT", [128, DR])
        nsin = sb("nsin", [128, DR // 2])
        psin = sb("psin", [128, DR // 2])
        causal = sb("causal", [128, 128])
        sel32 = sb("sel32", [128, NG])
        sel = sb("sel", [128, NG, 128], BF16)
        mean = sb("mean", [128, 128], BF16)
        neghalf = sb("neghalf", [128, 4])
        w_dqkv = sb("w_dqkv", [128, 2 * DL])
        w_dT = sb("w_dT", [DL, 2, 128])
        w_uq = sb("w_uq", [DL, H * DH + H * DR])
        w_ukv = sb("w_ukv", [DL, 2 * H * DH])
        w_mla = sb("w_mla", [128, MEND])
        w_raw = sb("w_raw", [128, 4, D])
        w_x1 = sb("w_x1", [128, 2, D])
        w_x2 = sb("w_x2", [128, 2, D])
        w_o = sb("w_o", [128, 3, D])
        w_f1 = sb("w_f1", [128, FF])
        w_f2 = sb("w_f2", [128, FF // 128, D])
        b_f1 = sb("b_f1", [128, FF // 128])
        b_f2 = sb("b_f2", [128, 1])
        gb = sb("gb", [128, 6, D])
        w_rt = sb("w_rt", [E, D])
        w_r = sb("w_r", [128, E])
        b_r = sb("b_r", [128, E])
        w_e = sb("w_e", [128, E, D])
        mask_rows = sb("mask_rows", [128, B, SC], U8)
        mask_b = sb("mask_b", [B, SC], U8)
        mask_f = sb("mask_f", [B, SC])
        keep = sb("keep", [SC, B])
        maskbias = sb("maskbias", [SC, B])
        mask_terms = T[:].rearrange("p b t -> p (b t)")[:, 0:B * SC // 2].bitcast(BF16).rearrange(
            "p (b t) -> p b t", b=B)
        st6 = sb("st6", [128, 2, 6])
        mv = sb("mv", [128, 2, 2])
        veps = sb("veps", [128, 2])
        rstd = sb("rstd", [128, 2])
        xn = sb("xn", [128, 2, D])
        cx = sb("cx", [SC, 2, D])
        xnT = sb("xnT", [128, 2, 256])
        kf = sb("kf", [128, 2, H * DH])
        rt1 = sb("rt1", [128, 2, H + 1, DR])
        rt2 = sb("rt2", [128, 2, H + 1, DR])
        rr = sb("rr", [128, 2, H + 1, DR])
        QK = sb("QK", [128, 2, 3, H, 32], F16)
        QKT = sb("QKT", [128, 2, 3, NG, 128], F16)
        V = sb("V", [128, 2, H, 32])
        negm = sb("negm", [128, 2, NJ, 32], BF16)
        mT = sb("mT", [128, 2, 128], BF16)
        nmr = sb("nmr", [128, 2, SC], BF16)
        P = sb("P", [128, 2, NJ, NG, 128])
        OT = sb("OT", [128, 2, NG * 128])
        rden = sb("rden", [128, 2, H])
        O = sb("O", [128, 2, D])
        OTT = sb("OTT", [128, 2, 128])
        st6c = sb("st6c", [128, 2, 6])
        mvc = sb("mvc", [128, 2, 2])
        vepsc = sb("vepsc", [128, 2])
        rstdc = sb("rstdc", [128, 2])
        r0 = sb("r0", [128, 2, D])
        r1 = sb("r1", [128, 2, D])
        r2 = sb("r2", [128, 2, D])

        SS = ps("SS", [128, NJ, NG, 128])
        B0 = ps("B0", [128, 512])
        B1 = ps("B1", [128, 2, NG, 128], F16)
        B2 = ps("B2", [128, 512])
        B3 = ps("B3", [128, 512])
        B1f = B1[:].rearrange("r t g k -> r (t g k)").bitcast(F32)
        B3b = B3[:, 256:320].bitcast(BF16)
        B3k = B3[:, 128:384].bitcast(F16)

        s_x0, s_x1 = sem("x_first"), sem("x_rest")
        s_c, s_w, s_w2, s_m = (sem(n) for n in
                               ("consts_loaded", "mla_weights_loaded", "weights_loaded", "mask_loaded"))
        s_init, s_small = sem("init_done"), sem("small_transposed")
        s_wt, s_wtc, s_wf, s_wfc = (sem(n) for n in
                                    ("wd_transposed", "wd_copied", "wf_product", "wf_copied"))
        s_mr, s_prep2, s_prep = sem("mask_terms"), sem("later_weights_ready"), sem("weights_ready")
        per_batch = {
            "stats": (1, 1, 0), "aggr": (1, 1, 0), "veps": (1, 1, 0), "rstd": (1, 1, 0), "xn": (1, 1, 1),
            "xnT_ps": (1, 1, 1), "xnT": (1, 1, 1), "proj": (1, 1, 1), "v": (1, 1, 1), "kf": (0, 0, 1),
            "hi": (1, 2, 2), "lo": (1, 1, 1), "t1": (1, 0, 0), "rot": (1, 0, 0), "rhi": (1, 0, 0),
            "kb": (1, 0, 0), "kbT_ps": (1, 0, 0), "kbT": (1, 0, 0), "qkT_ps": (1, 1, 1), "qkT": (1, 1, 1), "nm": (0, 1, 1),
            "S": (0, 2, 2), "max": (0, 2, 2), "mT_ps": (0, 1, 1), "mT": (0, 1, 1), "ST": (2, 2, 2),
            "exp": (2, 2, 2), "clip": (2, 0, 0), "PV": (1, 1, 1), "OT": (1, 1, 1), "OTt": (1, 1, 1),
            "rden": (1, 1, 1), "O": (1, 1, 1), "O_ps": (1, 1, 1), "OTT": (1, 1, 1), "wo": (1, 1, 1),
            "took": (1, 1, 1), "statsc": (0, 1, 1), "aggrc": (0, 1, 1), "vepsc": (0, 1, 1),
            "rstdc": (0, 1, 1), "nrm": (0, 1, 1), "gain": (0, 1, 1), "done": (0, 1, 1)}
        attn_sem = {n: sem(f"attn_{n}") for n in per_batch}
        sems = [{n: Signal(attn_sem[n], B * sum(c[:k])) for n, c in per_batch.items()} for k in range(3)]
        s_ctx = [sem("ctx_loaded0"), sem("ctx_loaded1")]

        NW2 = 4 + 2 + 4 + 6 + 3

        block = ctx.enter_context(nc.Block())


        def pe_step(pe, p, norm, proj, soft, vals, outp):
            q = 1 - p

            def score_pass(k, s, m, nk):
                if k == MLA:
                    pe.wait_ge(m["qkT"].sem, m["qkT"].at(s + 1))
                    pe.wait_ge(m["kbT"].sem, m["kbT"].at(s + 1))
                    pe.wait_ge(m["exp"].sem, m["exp"].at(2 * s))
                else:
                    pe.wait_ge(m["mT"].sem, m["mT"].at(s + 1))
                for u in range(2):
                    for g in range(NG):
                        for j in (2 * u, 2 * u + 1):
                            if k == MLA:
                                r = slice(32 * j, 32 * j + ROWS_MLA)
                                pe.matmul(SS[:, j, g, :], QKT[r, p, 1, g, :], QKT[r, p, 0, g, :],
                                          start=True, stop=False)
                                mm = pe.matmul(SS[:, j, g, :], QKT[r, p, 2, g, :], QKT[r, p, 0, g, :],
                                               start=False, stop=True)
                            else:
                                r = slice(32 * j, 32 * j + 32)
                                pe.matmul(SS[0:nk, j, g, :], sel[32 * j:32 * j + NG, g, 0:nk],
                                          mT[32 * j:32 * j + NG, p, :], start=True, stop=False)
                                mm = pe.matmul(SS[0:nk, j, g, :], QKT[r, p, 1, g, 0:nk], QKT[r, p, 0, g, :],
                                               start=False, stop=True)
                    mm.then_inc(m["ST"].sem, 1)

            if proj:
                k, s = proj
                m, nk = sems[k], SC if k == CA else S
                pe.wait_ge(m["xn"].sem, m["xn"].at(s + 2))
                pe.wait_ge(m["xnT"].sem, m["xnT"].at(s + 1))
                if k == MLA:
                    pe.wait_ge(m["kbT"].sem, m["kbT"].at(s + 1))
                if k == SA and isinstance(s, int):
                    pe.wait_ge(sems[MLA]["kbT"].sem, sems[MLA]["kbT"].at(B))
                if k != MLA:
                    pe.wait_ge(m["mT"].sem, m["mT"].at(s))
                pe.wait_ge(m["OTT"].sem, m["OTT"].at(s - 2))
                if k == CA:
                    pe.wait_ge(s_ctx[q], 8 * (s + 1 - q) + 16)
                    pe.transpose(B3[:, 128:128 + nk], cx[:, q, :], id32[0:nk, 0:nk])
                pe.transpose(B3[:, 0:128], xn[:, q, :], id32[:]).then_inc(m["xnT_ps"].sem, 1)
            if outp:
                k, s = outp
                m = sems[k]
                pe.wait_ge(m["O"].sem, m["O"].at(s - 1))
                if not proj:
                    pe.wait_ge(m["OTT"].sem, m["OTT"].at(s - 2))
                    pe.wait_ge(m["mT"].sem, m["mT"].at(B if not soft else s))
                    pe.wait_ge(m["xnT"].sem, m["xnT"].at(B))
                pe.transpose(B3[:, 384:512], O[:, p, :], id32[:]).then_inc(m["O_ps"].sem, 1)
            if soft and soft[0] != MLA:
                k, s = soft
                m, nk = sems[k], SC if k == CA else S
                pe.wait_ge(m["qkT"].sem, m["qkT"].at(s + 1))
                if k == SA and isinstance(s, int):
                    pe.wait_ge(sems[MLA]["exp"].sem, sems[MLA]["exp"].at(2 * B))
                if k == CA:
                    pe.wait_ge(m["nm"].sem, m["nm"].at(s + 1))
                for u in range(2):
                    pe.wait_ge(m["exp"].sem, m["exp"].at(2 * s + u - 1))
                    if k == CA:
                        for j in (2 * u, 2 * u + 1):
                            pe.matmul(SS[:, j, :, 0:nk], mean[:],
                                      nmr[:, p, :].unsqueeze(1).broadcast_to([128, NG, nk]),
                                      start=True, stop=False)
                    for g in range(NG):
                        for j in (2 * u, 2 * u + 1):
                            r = slice(32 * j, 32 * j + 32)
                            mm = pe.matmul(SS[:, j, g, 0:nk], QKT[r, p, 0, g, :], QKT[r, p, 1, g, 0:nk],
                                           start=(k != CA), stop=(k != CA or g == NG - 1))
                    mm.then_inc(m["S"].sem, 1)
            if soft and soft[0] == MLA:
                score_pass(*soft, sems[MLA], S)
            if proj:
                k, s = proj
                m, nk = sems[k], SC if k == CA else S
                pe.wait_ge(m["xnT"].sem, m["xnT"].at(s + 2))
                pe.wait_ge(m["v"].sem, m["v"].at(s + 1))
                if k == MLA:
                    pe.matmul(B0[:, 0:MEND], xnT[:, q, 0:128], w_mla[:], start=True, stop=True
                              ).then_inc(m["proj"].sem, 1)
                elif k == SA:
                    pe.matmul(B0[:, 0:256], xnT[:, q, 0:128], w_x1[:].rearrange("p a n -> p (a n)"),
                              start=True, stop=True).then_inc(m["proj"].sem, 1)
                else:
                    pe.matmul(B0[:, 0:128], xnT[:, q, 0:128], w_x2[:, 0, :], start=True, stop=True)
                    pe.matmul(B0[0:nk, 128:256], xnT[:, q, 128:128 + nk], w_x2[:, 1, :],
                              start=True, stop=True).then_inc(m["proj"].sem, 1)
            if outp:
                k, s = outp
                m = sems[k]
                pe.wait_ge(m["OTT"].sem, m["OTT"].at(s - 1))
                if soft:
                    pe.wait_ge(sems[soft[0]]["qkT"].sem, sems[soft[0]]["qkT"].at(soft[1] + 1))
                pe.matmul(B1f[:, 0:128], OTT[:, p, :], w_o[:, k, :], start=True, stop=True
                          ).then_inc(m["wo"].sem, 1)
            if vals:
                k, s = vals
                m, nk = sems[k], SC if k == CA else S
                done = m["clip"] if k == MLA else m["exp"]
                pe.wait_ge(m["v"].sem, m["v"].at(s))
                pe.wait_ge(m["O"].sem, m["O"].at(s - 1))
                for u in range(2):
                    pe.wait_ge(done.sem, done.at(2 * s + u - 1))
                    for g in range(NG):
                        for j in (2 * u, 2 * u + 1):
                            mm = pe.matmul(B2[32 * j:32 * j + 32, g * 128:(g + 1) * 128],
                                           V[0:nk, q, 4 * g + j, :], P[0:nk, q, j, g, :],
                                           start=True, stop=True)
                mm.then_inc(m["PV"].sem, 1)
            if soft and soft[0] != MLA:
                k, s = soft
                m = sems[k]
                pe.wait_ge(m["max"].sem, m["max"].at(2 * s + 2))
                pe.wait_ge(m["xnT"].sem, m["xnT"].at(s + 2 if proj and proj[0] == k else B))
                if outp:
                    pe.wait_ge(sems[outp[0]]["OTT"].sem, sems[outp[0]]["OTT"].at(outp[1] - 1))
                pe.transpose(B3b, negm[:, p].rearrange("t j r -> t (j r)"), idb[:]).then_inc(m["mT_ps"].sem, 1)
            if proj:
                k, s = proj
                m, nk = sems[k], SC if k == CA else S
                pe.wait_ge(m["lo"].sem, m["lo"].at(s + 2))
                if outp:
                    pe.wait_ge(sems[outp[0]]["took"].sem, sems[outp[0]]["took"].at(outp[1] - 1))
                for t in range(2):
                    n = 128 if t == 0 else nk
                    for g in range(NG):
                        mm = pe.transpose(B1[:, t, g, 0:n],
                                          QK[0:n, q, t, 4 * g:4 * g + 4, :].rearrange("t h r -> t (h r)"),
                                          id16[0:n, 0:n])
                mm.then_inc(m["qkT_ps"].sem, 1)
            if vals:
                k, s = vals
                m = sems[k]
                pe.wait_ge(m["OT"].sem, m["OT"].at(s))
                for g in range(NG):
                    mm = pe.transpose(B2[:, g * 128:(g + 1) * 128], OT[:, q, g * 128:(g + 1) * 128], id32[:])
                mm.then_inc(m["OTt"].sem, 1)
            if soft and soft[0] != MLA:
                score_pass(*soft, sems[soft[0]], SC if soft[0] == CA else S)
            if proj and proj[0] == MLA:
                k, s = proj
                m = sems[k]
                pe.wait_ge(m["kb"].sem, m["kb"].at(s + 2))
                if outp:
                    pe.wait_ge(m["OTT"].sem, m["OTT"].at(s - 1))
                for g in range(NG):
                    mm = pe.transpose(B3k[:, g * 128:(g + 1) * 128],
                                      QK[:, q, 2, 4 * g:4 * g + 4, :].rearrange("t h r -> t (h r)"), id16[:])
                mm.then_inc(m["kbT_ps"].sem, 1)

        def act_step(act, p, norm, proj, soft, vals, outp):
            q = 1 - p

            def exps(k, s, u):
                m, nk = sems[k], SC if k == CA else S
                act.wait_ge(m["ST"].sem, m["ST"].at(2 * s + u + 1))
                act.wait_ge(m["PV"].sem, m["PV"].at(s - 1))
                o = P[0:nk, p, 2 * u:2 * u + 2].rearrange("k j g q -> k (j g q)")
                src = SS[0:nk, 2 * u:2 * u + 2].rearrange("k j g q -> k (j g q)")
                if k == CA:
                    apart(act)
                    act.activation(o, src, ACT.Exp, bias=maskbias[:, bass.ds(s, 1)], scale=SCALE_X
                                   ).then_inc(m["exp"].sem, 1)
                else:
                    act.activation(o, src, ACT.Exp, scale=SCALE_MLA if k == MLA else SCALE_X
                                   ).then_inc(m["exp"].sem, 1)

            if proj:
                k, s = proj
                m, nk = sems[k], SC if k == CA else S
                act.wait_ge(m["xnT_ps"].sem, m["xnT_ps"].at(s + 2))
                if outp:
                    act.wait_ge(sems[outp[0]]["O_ps"].sem, sems[outp[0]]["O_ps"].at(outp[1] - 1))
                act.wait_ge(m["proj"].sem, m["proj"].at(s))
                n = 128 + nk if k == CA else 128
                act.activation(xnT[:, q, 0:n], B3[:, 0:n], ACT.Copy).then_inc(m["xnT"].sem, 1)
            if outp:
                k, s = outp
                m = sems[k]
                act.wait_ge(m["O_ps"].sem, m["O_ps"].at(s - 1))
                act.wait_ge(m["wo"].sem, m["wo"].at(s - 3))
                act.activation(OTT[:, p, :], B3[:, 384:512], ACT.Copy).then_inc(m["OTT"].sem, 1)
            if soft and soft[0] == MLA:
                for u in range(2):
                    exps(*soft, u)
            if proj:
                k, s = proj
                m, nk = sems[k], SC if k == CA else S
                act.wait_ge(m["proj"].sem, m["proj"].at(s + 2))
                act.wait_ge(m["qkT_ps"].sem, m["qkT_ps"].at(s))
                if k == MLA:
                    act.wait_ge(m["kb"].sem, m["kb"].at(s))
                if k == MLA:
                    act.activation(QK[:, q, 0:2, :, 0:DH],
                                   B0[:, 0:MV].rearrange("t (a h d) -> t a h d", a=2, d=DH),
                                   ACT.Copy).then_inc(m["hi"].sem, 1)
                else:
                    qv = B0[:, 0:128].rearrange("t (h o d) -> t h o d", o=1, d=DH).broadcast_to([128, H, 2, DH])
                    act.activation(QK[:, q, 0, :, 0:2 * DH].rearrange("t h (r d) -> t h r d", r=2), qv,
                                   ACT.Copy).then_inc(m["hi"].sem, 1)
                    if k == CA:
                        act.wait_ge(m["lo"].sem, m["lo"].at(s))
                        apart(act)
                        act.activation(kf[0:nk, q, :], B0[0:nk, 128:256], ACT.Copy,
                                       scale=keep[:, bass.ds(s + 1, 1)]).then_inc(m["kf"].sem, 1)
                    if k == CA:
                        act.wait_ge(m["kf"].sem, m["kf"].at(s + 2))
                        src = kf[0:nk, q, :]
                    else:
                        src = B0[0:nk, 128:256]
                    act.activation(QK[0:nk, q, 1].rearrange("t h (r z d) -> t h r z d", r=2, z=2)[:, :, :, 0, :],
                                   src.rearrange("t (h o d) -> t h o d", o=1, d=DH).broadcast_to([nk, H, 2, DH]),
                                   ACT.Copy).then_inc(m["hi"].sem, 1)
            if vals:
                k, s = vals
                m = sems[k]
                act.wait_ge(m["PV"].sem, m["PV"].at(s))
                act.wait_ge(m["OTt"].sem, m["OTt"].at(s - 2))
                act.activation(OT[:, q, :], B2[:], ACT.Copy).then_inc(m["OT"].sem, 1)
            if proj:
                k, s = proj
                m, nk = sems[k], SC if k == CA else S
                act.wait_ge(m["PV"].sem, m["PV"].at(s))
                act.wait_ge(m["lo"].sem, m["lo"].at(s + 2))
                x = B0[0:nk, MV:MR] if k == MLA else B0[0:nk, 128:256]
                act.activation(V[0:nk, q, :, 0:DH], x.rearrange("t (h d) -> t h d", d=DH),
                               ACT.Copy).then_inc(m["v"].sem, 1)
            if proj and proj[0] == MLA:
                k, s = proj
                m = sems[k]
                act.wait_ge(m["lo"].sem, m["lo"].at(s + 2))
                act.wait_ge(m["kbT_ps"].sem, m["kbT_ps"].at(s))
                h = DH + DR
                act.activation(QK[:, q, 2, :, 0:h], QK[:, q, 1, :, h:2 * h], ACT.Copy)
                act.activation(QK[:, q, 2, :, h:2 * h], QK[:, q, 1, :, 0:h], ACT.Copy).then_inc(m["kb"].sem, 1)
            if soft and soft[0] != MLA:
                for u in range(2):
                    exps(*soft, u)
            if proj and proj[0] == MLA:
                k, s = proj
                m = sems[k]
                act.wait_ge(m["kbT_ps"].sem, m["kbT_ps"].at(s + 2))
                act.wait_ge(m["ST"].sem, m["ST"].at(2 * s))
                act.activation(QKT[:, q, 2].rearrange("r g k -> r (g k)"), B3k, ACT.Copy).then_inc(m["kbT"].sem, 1)

        def dve_step(v, p, norm, proj, soft, vals, outp):
            q = 1 - p

            def clip(s, u):
                m = sems[MLA]
                v.wait_ge(m["exp"].sem, m["exp"].at(2 * s + u + 1))
                for j in (2 * u, 2 * u + 1):
                    ins = v.scalar_tensor_tensor(P[:, p, j], P[:, p, j], P_LO,
                                                 causal[:].unsqueeze(1).broadcast_to([128, NG, 128]),
                                                 ALU.max, ALU.min)
                ins.then_inc(m["clip"].sem, 1)

            if norm and norm[0] != CA:
                k, s = norm
                m = sems[k]
                if k == SA and isinstance(s, int):
                    v.wait_ge(sems[MLA]["took"].sem, sems[MLA]["took"].at(s + 3))
                v.wait_ge(m["aggr"].sem, m["aggr"].at(s + 1))
                apart(v)
                v.bn_stats(st6[:, p, :], X[:, s + 2, :]).then_inc(m["stats"].sem, 1)
            if norm and norm[0] != CA:
                k, s = norm
                m = sems[k]
                v.wait_ge(m["stats"].sem, m["stats"].at(s + 3))
                v.wait_ge(m["xn"].sem, m["xn"].at(s + 1))
                apart(v)
                v.bn_aggr(mv[:, p, :], st6[:, p, :]).then_inc(m["aggr"].sem, 1)
            if soft and soft[0] == MLA:
                clip(soft[1], 0)
            if soft and soft[0] != MLA:
                k, s = soft
                m, nk = sems[k], SC if k == CA else S
                for u in range(2):
                    v.wait_ge(m["S"].sem, m["S"].at(2 * s + u + 1))
                    v.wait_ge(m["mT_ps"].sem, m["mT_ps"].at(s - 1))
                    v.tensor_reduce(negm[:, p, 2 * u:2 * u + 2, 0:NG], SS[:, 2 * u:2 * u + 2, :, 0:nk],
                                    AX, ALU.max, negate=True).then_inc(m["max"].sem, 1)
            if outp:
                k, s = outp
                m, i = sems[k], s - 2
                v.wait_ge(m["wo"].sem, m["wo"].at(s - 1))
                if k == MLA:
                    v.tensor_tensor(X[:, i, :], B1f[:, 0:128], X[:, i, :], ALU.add).then_inc(m["took"].sem, 1)
                else:
                    v.wait_ge(m["nrm"].sem, m["nrm"].at(s - 3))
                    if k == SA:
                        v.wait_ge(m["nm"].sem, m["nm"].at(s - 1))
                    v.tensor_tensor(r0[:, p, :], B1f[:, 0:128], Y[:, i, :], ALU.add).then_inc(m["took"].sem, 1)
            if proj:
                k, s = proj
                m, nk = sems[k], SC if k == CA else S
                v.wait_ge(m["hi"].sem, m["hi"].at((1 if k == MLA else 2) * (s + 2)))
                if k == MLA:
                    x = B0[:, MR:MEND].rearrange("t (h d) -> t h d", d=DR)
                    x2 = B0[:, MR:MEND].rearrange("t (h c e) -> t h c e", e=2, c=DR // 2)
                    y2 = rt2[:, q].rearrange("t h (c e) -> t h c e", e=2)
                    n = [128, H + 1, DR // 2]
                    v.wait_ge(m["rot"].sem, m["rot"].at(s))
                    v.tensor_tensor(rt1[:, q], x, cosT[:].unsqueeze(1).broadcast_to([128, H + 1, DR]), ALU.mult)
                    v.tensor_tensor(y2[:, :, :, 0], x2[:, :, :, 1], nsin[:].unsqueeze(1).broadcast_to(n), ALU.mult)
                    v.tensor_tensor(y2[:, :, :, 1], x2[:, :, :, 0], psin[:].unsqueeze(1).broadcast_to(n),
                                    ALU.mult).then_inc(m["t1"].sem, 1)
                    v.tensor_tensor(QK[:, q, 0:2, :, DH + DR:2 * DH + DR],
                                    B0[:, 0:MV].rearrange("t (a h d) -> t a h d", a=2, d=DH),
                                    QK[:, q, 0:2, :, 0:DH], ALU.subtract)
                    v.wait_ge(m["t1"].sem, m["t1"].at(s + 2))
                    v.wait_ge(m["lo"].sem, m["lo"].at(s))
                    v.tensor_tensor(rr[:, q], rt1[:, q], rt2[:, q], ALU.add).then_inc(m["rot"].sem, 1)
                    v.wait_ge(m["rot"].sem, m["rot"].at(s + 2))
                    qr = rr[:, q, 0:H, :]
                    kr = rr[:, q, H:H + 1, :].broadcast_to([128, H, DR])
                    v.tensor_copy(QK[:, q, 0, :, DH:DH + DR], qr)
                    v.tensor_copy(QK[:, q, 1, :, DH:DH + DR], kr).then_inc(m["rhi"].sem, 1)
                    v.wait_ge(m["rhi"].sem, m["rhi"].at(s + 2))
                    v.tensor_tensor(QK[:, q, 0, :, 2 * DH + DR:ROWS_MLA], qr, QK[:, q, 0, :, DH:DH + DR],
                                    ALU.subtract)
                    v.tensor_tensor(QK[:, q, 1, :, 2 * DH + DR:ROWS_MLA], kr, QK[:, q, 1, :, DH:DH + DR],
                                    ALU.subtract).then_inc(m["lo"].sem, 1)
                else:
                    ksrc = kf[0:nk, q, :] if k == CA else B0[0:nk, 128:256]
                    bc = lambda z, n: z.rearrange("t (h o d) -> t h o d", o=1, d=DH).broadcast_to([n, H, 2, DH])
                    v.tensor_tensor(QK[:, q, 0, :, 2 * DH:32].rearrange("t h (r d) -> t h r d", r=2),
                                    bc(B0[:, 0:128], 128),
                                    QK[:, q, 0, :, 0:2 * DH].rearrange("t h (r d) -> t h r d", r=2),
                                    ALU.subtract)
                    kv = QK[0:nk, q, 1].rearrange("t h (r z d) -> t h r z d", r=2, z=2)
                    v.tensor_tensor(kv[:, :, :, 1, :], bc(ksrc, nk), kv[:, :, :, 0, :],
                                    ALU.subtract).then_inc(m["lo"].sem, 1)
            if soft and soft[0] == MLA:
                clip(soft[1], 1)
            if soft and soft[0] != MLA:
                k, s = soft
                m = sems[k]
                v.wait_ge(m["mT_ps"].sem, m["mT_ps"].at(s + 1))
                v.wait_ge(m["ST"].sem, m["ST"].at(2 * s - 2))
                v.tensor_copy(mT[:, p, :], B3b).then_inc(m["mT"].sem, 1)
            if proj:
                k, s = proj
                m, nk = sems[k], SC if k == CA else S
                v.wait_ge(m["qkT_ps"].sem, m["qkT_ps"].at(s + 2))
                v.wait_ge(m["ST"].sem, m["ST"].at(2 * s))
                if k == CA:
                    v.tensor_copy(QKT[:, q, 0].rearrange("r g k -> r (g k)"), B1[:, 0].rearrange("r g k -> r (g k)"))
                    v.tensor_copy(QKT[:, q, 1, :, 0:nk], B1[:, 1, :, 0:nk]).then_inc(m["qkT"].sem, 1)
                else:
                    v.tensor_copy(QKT[:, q, 0:2].rearrange("r t g k -> r (t g k)"),
                                  B1[:].rearrange("r t g k -> r (t g k)")).then_inc(m["qkT"].sem, 1)
            if outp and outp[0] != MLA:
                k, s = outp
                m = sems[k]
                v.wait_ge(m["took"].sem, m["took"].at(s - 1))
                v.wait_ge(m["aggrc"].sem, m["aggrc"].at(s - 3))
                apart(v)
                v.bn_stats(st6c[:, p, :], r0[:, p, :]).then_inc(m["statsc"].sem, 1)
            if norm and norm[0] != CA:
                k, s = norm
                m = sems[k]
                v.wait_ge(m["rstd"].sem, m["rstd"].at(s + 3))
                v.wait_ge(m["xnT_ps"].sem, m["xnT_ps"].at(s + 1))
                if k == SA:
                    v.wait_ge(m["nm"].sem, m["nm"].at(s + 1))
                v.tensor_scalar(xn[:, p, :], X[:, s + 2, :], mv[:, p, 0:1], rstd[:, p:p + 1],
                                ALU.subtract, ALU.mult).then_inc(m["xn"].sem, 1)
            if outp and outp[0] != MLA:
                k, s = outp
                m = sems[k]
                v.wait_ge(m["statsc"].sem, m["statsc"].at(s - 1))
                v.wait_ge(m["nrm"].sem, m["nrm"].at(s - 3))
                apart(v)
                v.bn_aggr(mvc[:, p, :], st6c[:, p, :]).then_inc(m["aggrc"].sem, 1)
            if vals:
                k, s = vals
                m = sems[k]
                v.wait_ge(m["OTt"].sem, m["OTt"].at(s))
                v.wait_ge(m["O"].sem, m["O"].at(s - 2))
                ot = B2[:].rearrange("t (h r) -> t h r", r=32)
                v.reciprocal(rden[:, q, :], ot[:, :, DH]).then_inc(m["rden"].sem, 1)
            if vals:
                k, s = vals
                m = sems[k]
                v.wait_ge(m["rden"].sem, m["rden"].at(s))
                v.wait_ge(m["O_ps"].sem, m["O_ps"].at(s - 2))
                o = (O[:, q, :].rearrange("t (h d) -> t h d", d=DH) if k == MLA
                     else O[:, q, :].rearrange("t (d h) -> t h d", d=DH))
                v.tensor_tensor(o, ot[:, :, 0:DH], rden[:, q, :].unsqueeze(2).broadcast_to([128, H, DH]),
                                ALU.mult).then_inc(m["O"].sem, 1)
            if outp and outp[0] != MLA:
                k, s = outp
                m = sems[k]
                v.wait_ge(m["rstdc"].sem, m["rstdc"].at(s - 1))
                v.wait_ge(m["gain"].sem, m["gain"].at(s - 3))
                v.tensor_scalar(r1[:, p, :], r0[:, p, :], mvc[:, p, 0:1], rstdc[:, p:p + 1],
                                ALU.subtract, ALU.mult).then_inc(m["nrm"].sem, 1)
            if outp and outp[0] != MLA:
                k, s = outp
                m = sems[k]
                v.wait_ge(m["nrm"].sem, m["nrm"].at(s - 1))
                v.wait_ge(m["done"].sem, m["done"].at(s - 3))
                v.tensor_tensor(r2[:, p, :], r1[:, p, :], gb[:, 2 * (k - 1), :], ALU.mult
                                ).then_inc(m["gain"].sem, 1)
            if outp and outp[0] != MLA:
                k, s = outp
                m = sems[k]
                v.wait_ge(m["gain"].sem, m["gain"].at(s - 1))
                v.tensor_tensor(Y[:, s - 2, :], r2[:, p, :], gb[:, 2 * (k - 1) + 1, :], ALU.add
                                ).then_inc(m["done"].sem, 1)

        def pool_step(po, p, norm, proj, soft, vals, outp):
            q = 1 - p
            if norm and norm[0] == CA:
                k, s = norm
                m = sems[k]
                if isinstance(s, int):
                    po.wait_ge(sems[SA]["done"].sem, sems[SA]["done"].at(s + 3))
                po.wait_ge(m["xnT_ps"].sem, m["xnT_ps"].at(s + 1))
                apart(po)
                po.tensor_copy(xn[:, p, :], Y[:, s + 2, :]).then_inc(m["xn"].sem, 1)
            if norm and norm[0] != CA:
                k, s = norm
                m = sems[k]
                po.wait_ge(m["aggr"].sem, m["aggr"].at(s + 3))
                po.wait_ge(m["rstd"].sem, m["rstd"].at(s + 1))
                apart(po)
                po.tensor_scalar(veps[:, p:p + 1], mv[:, p, 1:2], LN_EPS, None, ALU.add).then_inc(m["veps"].sem, 1)
                po.wait_ge(m["veps"].sem, m["veps"].at(s + 3))
                po.wait_ge(m["xn"].sem, m["xn"].at(s + 1))
                po.tensor_tensor(rstd[:, p:p + 1], veps[:, p:p + 1], neghalf[:, 1:2], ALU.pow
                                 ).then_inc(m["rstd"].sem, 1)
            if outp and outp[0] != MLA:
                k, s = outp
                m = sems[k]
                po.wait_ge(m["aggrc"].sem, m["aggrc"].at(s - 1))
                po.wait_ge(m["rstdc"].sem, m["rstdc"].at(s - 3))
                apart(po)
                po.tensor_scalar(vepsc[:, p:p + 1], mvc[:, p, 1:2], LN_EPS, None, ALU.add
                                 ).then_inc(m["vepsc"].sem, 1)
                po.wait_ge(m["vepsc"].sem, m["vepsc"].at(s - 1))
                po.wait_ge(m["nrm"].sem, m["nrm"].at(s - 3))
                po.tensor_tensor(rstdc[:, p:p + 1], vepsc[:, p:p + 1], neghalf[:, 1:2], ALU.pow
                                 ).then_inc(m["rstdc"].sem, 1)
            if norm and norm[0] == SA:
                k, s = norm
                m = sems[k]
                po.wait_ge(m["xn"].sem, m["xn"].at(s + 3))
                apart(po)
                po.tensor_copy(Y[:, s + 2, :], xn[:, p, :]).then_inc(m["nm"].sem, 1)
            if norm and norm[0] == CA:
                k, s = norm
                m = sems[k]
                po.wait_ge(m["S"].sem, m["S"].at(2 * (s + 1)))
                apart(po)
                po.tensor_copy(nmr[:, p, :], mask_terms[:, s + 2, :]).then_inc(m["nm"].sem, 1)

        def seam(eng, step, k):
            for s in range(-2, 2):
                pieces = []
                for ahead in (2, 1, 0, -1, -2):
                    kk = k if s + ahead >= 0 else k - 1
                    pieces.append((kk, s if kk == k else s + B) if 0 <= kk <= CA else None)
                step(eng, s % 2, *pieces)

        def steady(eng, step, k):
            with eng.Fori(1, B // 2 - 1) as t:
                for p in range(2):
                    at = (k, 2 * t + p)
                    step(eng, p, at, at, at, at, at)

        fn = ["y", "yT_ps", "yT", "h_ps", "h", "o_ps", "o", "b_ps", "r", "st", "ag", "ve", "rs", "n", "g",
              "f", "x2", "st2", "ag2", "ve2", "rs2", "n2", "t_ps", "t", "l_ps", "l"]
        f = {n: Signal(sem(f"mlp_{n}")) for n in fn}
        yb = sb("yb", [128, 2, QW, D])
        yT = sb("yT", [128, 2, QW * 128])
        hT = P[:].rearrange("p a j g q -> p a j (g q)")
        oT = OT
        rb = sb("rb", [128, QW, D])
        nb = sb("nb", [128, QW, D])
        t2 = sb("t2", [128, QW, D])
        st24 = sb("st24", [128, QW, 6])
        mv8 = sb("mv8", [128, QW, 2])
        ve4 = sb("ve4", [128, QW])
        rs4 = sb("rs4", [128, QW])
        NHC = FF // 128

        tT = QKT[:].rearrange("r a t g k -> r (a t g k)").bitcast(F32)[:, 0:2 * QW * 128].rearrange(
            "r (a n) -> r a n", a=2)

        def pipeline(eng, step, ahead, behind):
            head = -ahead
            first = behind + (behind + ahead) % 2 + (ahead % 2)
            first += first % 2
            last = (NQ - ahead) // 2 * 2
            for s in range(head, first):
                step(eng, s, s % 2, lambda d, s=s: 0 <= s + d < NQ)
            with eng.Fori(first // 2, last // 2) as t:
                for p in range(2):
                    step(eng, 2 * t + p, p, lambda d: True)
            for s in range(last, NQ + behind):
                step(eng, s, s % 2, lambda d, s=s: 0 <= s + d < NQ)


        def mlp_pool_step(po, s, p, runs):
            q = 1 - p
            if runs(1):
                po.wait_ge(f["yT_ps"].sem, f["yT_ps"].at(s))
                po.tensor_copy(yb[:, q], Y[:, bass.ds(QW * (s + 1), QW), :]).then_inc(f["y"].sem, 1)
            if runs(-1):
                for ag, ve, rs in (("ag", "ve", "rs"), ("ag2", "ve2", "rs2")):
                    po.wait_ge(f[ag].sem, f[ag].at(s))
                    apart(po)
                    po.tensor_scalar(ve4[:], mv8[:, :, 1], LN_EPS, None, ALU.add).then_inc(f[ve].sem, 1)
                    po.wait_ge(f[ve].sem, f[ve].at(s))
                    po.tensor_tensor(rs4[:], ve4[:], neghalf[:, 1:2].broadcast_to([128, QW]), ALU.pow
                                     ).then_inc(f[rs].sem, 1)

        def mlp_pe_step(pe, s, p, runs):
            q = 1 - p
            if runs(1):
                pe.wait_ge(f["y"].sem, f["y"].at(s + 2))
                pe.wait_ge(f["l"].sem, f["l"].at(s - 2))
                pe.wait_ge(f["yT"].sem, f["yT"].at(s + 1))
                for b in range(QW):
                    mm = pe.transpose(B0[:, b * 128:(b + 1) * 128], yb[:, q, b, :], id32[:])
                mm.then_inc(f["yT_ps"].sem, 1)
            if runs(-1):
                pe.wait_ge(f["o"].sem, f["o"].at(s))
                pe.wait_ge(f["r"].sem, f["r"].at(s - 1))
                for b in range(QW):
                    mm = pe.transpose(B3[:, b * 128:(b + 1) * 128], oT[:, q, b * 128:(b + 1) * 128], id32[:])
                mm.then_inc(f["b_ps"].sem, 1)
            if runs(0):
                pe.wait_ge(f["yT"].sem, f["yT"].at(s + 1))
                for c in range(NHC):
                    pe.wait_ge(f["h"].sem, f["h"].at(NHC * s - NHC + c + 1))
                    pe.matmul(SS[:, c].rearrange("p g q -> p (g q)"), w_f1[:, c * 128:(c + 1) * 128],
                              yT[:, p, :], start=True, stop=True).then_inc(f["h_ps"].sem, 1)
            if runs(-2):
                pe.wait_ge(f["n2"].sem, f["n2"].at(s - 1))
                pe.wait_ge(f["t"].sem, f["t"].at(s - 2))
                for b in range(QW):
                    mm = pe.transpose(B1f[:, b * 128:(b + 1) * 128], t2[:, b, :], id32[:])
                mm.then_inc(f["t_ps"].sem, 1)
            if runs(0):
                pe.wait_ge(f["o"].sem, f["o"].at(s))
                for c in range(NHC):
                    pe.wait_ge(f["h"].sem, f["h"].at(NHC * s + c + 1))
                    mm = pe.matmul(B2[:], w_f2[:, c, :], hT[:, p, c, :], start=(c == 0), stop=(c == NHC - 1))
                mm.then_inc(f["o_ps"].sem, 1)
            if runs(-2):
                pe.wait_ge(f["t"].sem, f["t"].at(s - 1))
                if runs(1):
                    pe.wait_ge(f["yT"].sem, f["yT"].at(s + 2))
                else:
                    pe.wait_ge(f["l"].sem, f["l"].at(s - 2))
                for b in range(QW):
                    mm = pe.matmul(B0[:, b * E:(b + 1) * E], tT[:, p, b * 128:(b + 1) * 128], w_r[:],
                                   start=True, stop=True)
                mm.then_inc(f["l_ps"].sem, 1)

        def mlp_act_step(act, s, p, runs):
            q = 1 - p
            if runs(1):
                act.wait_ge(f["yT_ps"].sem, f["yT_ps"].at(s + 2))
                act.wait_ge(f["h_ps"].sem, f["h_ps"].at(NHC * s))
                act.activation(yT[:, q, :], B0[:], ACT.Copy).then_inc(f["yT"].sem, 1)
            if runs(0):
                for c in range(NHC):
                    act.wait_ge(f["h_ps"].sem, f["h_ps"].at(NHC * s + c + 1))
                    act.wait_ge(f["o_ps"].sem, f["o_ps"].at(s - 1))
                    act.activation(hT[:, p, c, :], SS[:, c].rearrange("p g q -> p (g q)"), ACT.Gelu,
                                   bias=b_f1[:, c:c + 1]).then_inc(f["h"].sem, 1)
            if runs(-2):
                act.wait_ge(f["t_ps"].sem, f["t_ps"].at(s - 1))
                act.wait_ge(f["l_ps"].sem, f["l_ps"].at(s - 3))
                act.activation(tT[:, p, :], B1f, ACT.Copy)
                act.activation(T[:, bass.ds(QW * (s - 2), QW), :], B1f.rearrange("p (b t) -> p b t", b=QW),
                               ACT.Copy).then_inc(f["t"].sem, 1)
            if runs(0):
                act.wait_ge(f["o_ps"].sem, f["o_ps"].at(s + 1))
                act.wait_ge(f["b_ps"].sem, f["b_ps"].at(s - 1))
                act.activation(oT[:, p, :], B2[:], ACT.Identity, bias=b_f2[:, 0:1]).then_inc(f["o"].sem, 1)

        def mlp_dve_step(v, s, p, runs):
            q = 1 - p

            def layer_norm(src, dst, n, st, ag, rs):
                apart(v)
                for b in range(QW):
                    ins = v.bn_stats(st24[:, b, :], src(b))
                ins.then_inc(f[st].sem, 1)
                v.wait_ge(f[st].sem, f[st].at(s))
                apart(v)
                for b in range(QW):
                    ins = v.bn_aggr(mv8[:, b, :], st24[:, b, :])
                ins.then_inc(f[ag].sem, 1)
                v.wait_ge(f[rs].sem, f[rs].at(s))
                for b in range(QW):
                    ins = v.tensor_scalar(dst[:, b, :], src(b), mv8[:, b, 0:1], rs4[:, b:b + 1],
                                          ALU.subtract, ALU.mult)
                ins.then_inc(f[n].sem, 1)

            if runs(-1):
                i = s - 1
                v.wait_ge(f["b_ps"].sem, f["b_ps"].at(s))
                v.tensor_tensor(rb[:], B3[:].rearrange("t (b d) -> t b d", b=QW), Y[:, bass.ds(QW * i, QW), :], ALU.add
                                ).then_inc(f["r"].sem, 1)
                v.wait_ge(f["r"].sem, f["r"].at(s))
                layer_norm(lambda b: rb[:, b, :], nb, "n", "st", "ag", "rs")
                v.wait_ge(f["n"].sem, f["n"].at(s))
                v.tensor_tensor(rb[:], nb[:], gb[:, 4:5, :].broadcast_to([128, QW, D]), ALU.mult
                                ).then_inc(f["g"].sem, 1)
                v.wait_ge(f["g"].sem, f["g"].at(s))
                v.tensor_tensor(nb[:], rb[:], gb[:, 5:6, :].broadcast_to([128, QW, D]), ALU.add
                                ).then_inc(f["f"].sem, 1)
                v.wait_ge(f["f"].sem, f["f"].at(s))
                xs = X[:, bass.ds(QW * i, QW), :]
                v.tensor_tensor(xs, xs, nb[:], ALU.add).then_inc(f["x2"].sem, 1)
                v.wait_ge(f["x2"].sem, f["x2"].at(s))
                v.wait_ge(f["t_ps"].sem, f["t_ps"].at(s - 1))
                layer_norm(lambda b: X[:, QW * i + b, :], t2, "n2", "st2", "ag2", "rs2")
            if runs(-2):
                v.wait_ge(f["l_ps"].sem, f["l_ps"].at(s - 1))
                v.tensor_tensor(L[:, bass.ds(QW * (s - 2), QW), :],
                                B0[:, 0:QW * E].rearrange("t (b e) -> t b e", e=E),
                                b_r[:].unsqueeze(1).broadcast_to([128, QW, E]), ALU.add).then_inc(f["l"].sem, 1)

        en = ["lm", "ld", "ex", "sm", "rc", "pr", "t8", "t8s", "mr", "sl", "gs", "s6", "s6e", "r6", "g1",
              "ga", "gm", "gr", "gate", "gp", "tb", "y", "acc", "sc", "p1", "p2", "p3", "out"]
        e = {n: Signal(sem(f"moe_{n}")) for n in en}
        e_st = [sem("moe_stored0"), sem("moe_stored1")]
        NA = 8
        ND = E - NA
        lm = sb("lm", [128, QW])
        le = sb("le", [128, QW, E])
        ssum = sb("ssum", [128, QW])
        p18 = sb("p18", [128, QW, E + 2])
        t8 = sb("t8", [128, QW, 8])
        mr = sb("mr", [128, QW, E + 2])
        gsel = sb("gsel", [128, QW, E])
        graw = sb("graw", [128, QW, E])
        g6 = sb("g6", [128, QW, 4])
        gate = sb("gate", [128, 2, QW, E])
        epsT = sb("epsT", [128, 2, QW])
        flat = P[:].rearrange("p a j g q -> p (a j g q)")
        n0, n1, n2 = 2 * QW * 128, 2 * NA * D, 2 * 4 * D
        tb = flat[:, 0:n0].rearrange("p (a b t) -> p a b t", a=2, b=QW)
        sc = flat[:, n0:n0 + n1].rearrange("p (a x d) -> p a x d", a=2, x=NA)
        padd = flat[:, n0 + n1:n0 + n1 + n2].rearrange("p (a x d) -> p a x d", a=2, x=4)
        acc = sb("acc", [128, 2, 2, D])
        psum3 = sb("psum3", [128, 2, D])
        ob = sb("ob", [128, 2, D])


        def moe_logits(v, s):
            v.wait_ge(e["gate"].sem, e["gate"].at(s))
            ls = L[:, bass.ds(QW * s, QW), :]
            v.tensor_reduce(lm[:], ls, AX, ALU.max).then_inc(e["lm"].sem, 1)
            v.wait_ge(e["lm"].sem, e["lm"].at(s + 1))
            v.tensor_tensor(le[:], ls, bc(lm[:]), ALU.subtract).then_inc(e["ld"].sem, 1)

        def bc(z):
            return z.unsqueeze(2).broadcast_to([128, QW, E])

        def moe_gates(v, s, p):
            v.wait_ge(e["ex"].sem, e["ex"].at(s + 1))
            v.tensor_reduce(ssum[:], le[:], AX, ALU.add).then_inc(e["sm"].sem, 1)
            v.wait_ge(e["sm"].sem, e["sm"].at(s + 1))
            v.reciprocal(lm[:], ssum[:]).then_inc(e["rc"].sem, 1)
            v.wait_ge(e["rc"].sem, e["rc"].at(s + 1))
            v.tensor_tensor(p18[:, :, 0:E], le[:], bc(lm[:]), ALU.mult).then_inc(e["pr"].sem, 1)
            v.wait_ge(e["pr"].sem, e["pr"].at(s + 1))
            apart(v)
            for b in range(QW):
                ins = v.max(t8[:, b, :], p18[:, b, 0:E])
            ins.then_inc(e["t8"].sem, 1)
            v.wait_ge(e["t8"].sem, e["t8"].at(s + 1))
            v.memset(t8[:, :, TOPK:8], -1.0).then_inc(e["t8s"].sem, 1)
            v.wait_ge(e["t8s"].sem, e["t8s"].at(s + 1))
            apart(v)
            for b in range(QW):
                ins = v.match_replace(mr[:, b, :], t8[:, b, :], p18[:, b, :], -2.0)
            ins.then_inc(e["mr"].sem, 1)
            v.wait_ge(e["mr"].sem, e["mr"].at(s + 1))
            v.tensor_scalar(gsel[:], mr[:, :, 0:E], -1.5, None, ALU.is_lt).then_inc(e["sl"].sem, 1)
            v.wait_ge(e["sl"].sem, e["sl"].at(s + 1))
            v.tensor_tensor(graw[:], gsel[:], p18[:, :, 0:E], ALU.mult).then_inc(e["gs"].sem, 1)
            v.wait_ge(e["gs"].sem, e["gs"].at(s + 1))
            v.tensor_reduce(g6[:, :, 0], graw[:], AX, ALU.add).then_inc(e["s6"].sem, 1)
            v.wait_ge(e["s6"].sem, e["s6"].at(s + 1))
            v.tensor_scalar(g6[:, :, 1], g6[:, :, 0], MOE_EPS, None, ALU.add).then_inc(e["s6e"].sem, 1)
            v.wait_ge(e["s6e"].sem, e["s6e"].at(s + 1))
            v.reciprocal(g6[:, :, 2], g6[:, :, 1]).then_inc(e["r6"].sem, 1)
            v.wait_ge(e["r6"].sem, e["r6"].at(s + 1))
            v.tensor_tensor(gsel[:], graw[:], bc(g6[:, :, 2]), ALU.mult).then_inc(e["g1"].sem, 1)
            v.wait_ge(e["g1"].sem, e["g1"].at(s + 1))
            v.tensor_reduce(g6[:, :, 3], gsel[:], AX, ALU.add).then_inc(e["ga"].sem, 1)
            v.wait_ge(e["ga"].sem, e["ga"].at(s + 1))
            v.tensor_scalar(epsT[:, p], g6[:, :, 3], MOE_EPS, None, ALU.mult)
            v.tensor_scalar(g6[:, :, 0], g6[:, :, 3], MOE_EPS, None, ALU.max).then_inc(e["gm"].sem, 1)
            v.wait_ge(e["gm"].sem, e["gm"].at(s + 1))
            v.reciprocal(g6[:, :, 1], g6[:, :, 0]).then_inc(e["gr"].sem, 1)
            v.wait_ge(e["gr"].sem, e["gr"].at(s + 1))
            v.wait_ge(e["sc"].sem, e["sc"].at(QW * (s - 1)))
            v.tensor_tensor(gate[:, p], gsel[:], bc(g6[:, :, 1]), ALU.mult).then_inc(e["gate"].sem, 1)

        def bank(b2, c):
            if b2 == 0:
                return SS[:, c].rearrange("p g q -> p (g q)")
            return (B0[:], B1f, B2[:], B3[:])[c]

        def moe_pe_step(pe, s, p, runs):
            if not runs(0):
                return
            pe.wait_ge(e["tb"].sem, e["tb"].at(s + 1))
            for b in range(QW):
                n = QW * s + b
                pe.wait_ge(e["acc"].sem, e["acc"].at(n - 1))
                pe.wait_ge(e["sc"].sem, e["sc"].at(n - 1))
                for c in (2, 0, 3, 1):
                    pe.matmul(bank(b % 2, c), tb[:, p, b, :],
                              w_e[:, 4 * c:4 * c + 4, :].rearrange("p e n -> p (e n)"),
                              start=True, stop=True).then_inc(e["y"].sem, 1)

        def moe_act_step(act, s, p, runs):
            if runs(1):
                act.wait_ge(e["ld"].sem, e["ld"].at(s + 2))
                act.activation(le[:], le[:], ACT.Exp).then_inc(e["ex"].sem, 1)
            if runs(0):
                act.wait_ge(e["gate"].sem, e["gate"].at(s + 1))
                for b in range(QW):
                    n = QW * s + b
                    act.wait_ge(e["p1"].sem, e["p1"].at(n - 1))
                    for x in range(NA):
                        ex = E - NA + x
                        if x % 4 == 0:
                            act.wait_ge(e["y"].sem, e["y"].at(4 * n + (1 if x == 0 else 3)))
                        ins = act.activation(sc[:, b % 2, x, :],
                                             bank(b % 2, ex // 4)[:, ex % 4 * D:(ex % 4 + 1) * D],
                                             ACT.Copy, scale=gate[:, p, b, ex:ex + 1])
                    ins.then_inc(e["sc"].sem, 1)

        def moe_pool_step(po, s, p, runs):
            q = 1 - p
            if runs(1):
                po.wait_ge(e["y"].sem, e["y"].at(4 * QW * s))
                apart(po)
                po.tensor_copy(tb[:, q], T[:, bass.ds(QW * (s + 1), QW), :]).then_inc(e["tb"].sem, 1)
            if runs(0):
                for b in range(QW):
                    n, b2 = QW * s + b, b % 2
                    po.wait_ge(e["sc"].sem, e["sc"].at(n + 1))
                    po.wait_ge(e["p3"].sem, e["p3"].at(n - 1))
                    po.tensor_tensor(padd[:, b2], sc[:, b2, 0:4], sc[:, b2, 4:8], ALU.add).then_inc(e["p1"].sem, 1)
                    po.wait_ge(e["p1"].sem, e["p1"].at(n + 1))
                    po.tensor_tensor(padd[:, b2, 0:2], padd[:, b2, 0:2], padd[:, b2, 2:4], ALU.add
                                     ).then_inc(e["p2"].sem, 1)
                    po.wait_ge(e["p2"].sem, e["p2"].at(n + 1))
                    po.wait_ge(e["out"].sem, e["out"].at(n - 1))
                    po.tensor_tensor(psum3[:, b2], padd[:, b2, 0], padd[:, b2, 1], ALU.add).then_inc(e["p3"].sem, 1)

        def moe_dve_step(v, s, p, runs):
            if runs(1):
                moe_logits(v, s + 1)
            if runs(0):
                v.wait_ge(e["gate"].sem, e["gate"].at(s + 1))
                for b in range(QW):
                    n, b2 = QW * s + b, b % 2
                    if b == 2 and runs(1):
                        moe_gates(v, s + 1, 1 - p)
                    for x in range(ND):
                        src = bank(b2, x // 4)[:, x % 4 * D:(x % 4 + 1) * D]
                        prev = X[:, n, :] if x == 0 else acc[:, b2, (x + 1) % 2, :]
                        if x % 4 == 0:
                            v.wait_ge(e["y"].sem, e["y"].at(4 * n + (2 if x == 0 else 4)))
                        if x:
                            v.wait_ge(e["gp"].sem, e["gp"].at((ND - 1) * n + x))
                        ins = v.scalar_tensor_tensor(acc[:, b2, x % 2, :], src, gate[:, p, b, x:x + 1], prev,
                                                     ALU.mult, ALU.add)
                        ins.then_inc((e["gp"] if x < ND - 1 else e["acc"]).sem, 1)
                    v.wait_ge(e["acc"].sem, e["acc"].at(n + 1))
                    v.wait_ge(e["p3"].sem, e["p3"].at(n + 1))
                    if not (isinstance(s, int) and n < 2):
                        v.wait_ge(e_st[b2], 8 * (n - b2))
                    v.scalar_tensor_tensor(ob[:, b2, :], acc[:, b2, (ND - 1) % 2, :], epsT[:, p, b:b + 1],
                                           psum3[:, b2], ALU.add, ALU.add).then_inc(e["out"].sem, 1)
            elif runs(1):
                moe_gates(v, s + 1, 1 - p)

        def moe_store(sp):
            with sp.Fori(0, B // 2) as t:
                for b2 in range(2):
                    sp.wait_ge(e["out"].sem, e["out"].at(2 * t + b2 + 1))
                    sp.dma_start(out[bass.ds(2 * t + b2, 1)].rearrange("o t d -> (o t) d"),
                                 ob[:, b2, :]).then_inc(e_st[b2], 16)
            for b2 in range(2):
                sp.wait_ge(e_st[b2], 16 * (B // 2))

        @block.vector
        def _(v):
            v.memset(QK[:].rearrange("p a t h r -> p (a t h r)").bitcast(F32), 0.0)
            v.memset(V[:], 0.0).then_inc(s_init, 1)
            v.wait_ge(s_init, 1)
            v.memset(V[:, :, :, DH:DH + 1], 1.0)
            v.memset(negm[:], 0.0)
            v.memset(mean[:], 1.0 / 128)
            v.memset(neghalf[:], -0.5)
            v.memset(p18[:], -1.0)
            v.wait_ge(s_c, 16 * 6)
            v.tensor_copy(id16[:], id32[:])
            v.tensor_copy(idb[:], id32[:])
            v.tensor_copy(sel[:], sel32[:].unsqueeze(2).broadcast_to([128, NG, 128])).then_inc(s_init, 1)
            v.wait_ge(s_wt, 1)
            v.tensor_copy(w_dT[:, 0, :], B0[0:DL, 0:128])
            v.tensor_copy(w_dT[:, 1, :], B0[0:DL, 128:256]).then_inc(s_wtc, 1)
            v.wait_ge(s_wf, 1)
            v.tensor_copy(w_mla[:, MQ:MK], B2[:, 0:128])
            v.tensor_copy(w_mla[:, MR:MR + H * DR], B2[:, 128:128 + H * DR])
            v.tensor_copy(w_mla[:, MK:MR], B3[:, 0:256]).then_inc(s_prep, 1)
            v.wait_ge(s_prep, 1)
            v.wait_ge(s_x0, 16)
            seam(v, dve_step, MLA)
            v.wait_ge(s_x1, 16 * 3)
            steady(v, dve_step, MLA)
            v.wait_ge(s_w2, 16 * NW2)
            for x, w in ((0, w_x1), (2, w_x2)):
                v.tensor_copy(w[:].rearrange("p a (h d) -> p a h d", d=DH),
                              w_raw[:, x:x + 2, :].rearrange("p a (d h) -> p a h d", d=DH))
            v.wait_ge(s_m, 32)
            v.tensor_copy(mask_f[:], mask_b[:]).then_inc(s_init, 1)
            v.wait_ge(s_small, 1)
            v.tensor_copy(w_r[:], B0[:, 256:256 + E])
            v.tensor_scalar(keep[:], B0[0:SC, 320:320 + B], -1.0, 1.0, ALU.mult, ALU.add)
            v.tensor_scalar(maskbias[:], B0[0:SC, 320:320 + B], MASKED * SCALE_X, None, ALU.mult
                            ).then_inc(s_prep2, 1)
            for k in (SA, CA):
                seam(v, dve_step, k)
                if k == SA:
                    v.wait_ge(sems[MLA]["took"].sem, sems[MLA]["took"].at(B))
                steady(v, dve_step, k)
            seam(v, dve_step, CA + 1)
            v.wait_ge(sems[CA]["done"].sem, sems[CA]["done"].at(B))
            pipeline(v, mlp_dve_step, 1, 2)
            v.wait_ge(f["l"].sem, f["l"].at(NQ))
            pipeline(v, moe_dve_step, 1, 0)

        def warm_up(pe, k):
            pe.wait_ge(sems[k]["v"].sem, sems[k]["v"].at(3))
            for _ in range(3):
                pe.matmul(B0[:, 0:MEND], id32[:], w_mla[:], start=True, stop=True)

        @block.tensor
        def _(pe):
            pe.wait_ge(s_c, 16 * 6)
            pe.wait_ge(s_w, 16 * 8)
            pe.transpose(B0[0:DL, 0:128], w_dqkv[:, 0:DL], id32[:])
            pe.transpose(B0[0:DL, 128:256], w_dqkv[:, DL:2 * DL], id32[:]).then_inc(s_wt, 1)
            pe.wait_ge(s_wtc, 1)
            pe.matmul(B2[:, 0:192], w_dT[:, 0, :], w_uq[:], start=True, stop=True)
            pe.matmul(B3[:, 0:256], w_dT[:, 1, :], w_ukv[:], start=True, stop=True).then_inc(s_wf, 1)
            pe.wait_ge(s_prep, 1)
            seam(pe, pe_step, MLA)
            warm_up(pe, MLA)
            steady(pe, pe_step, MLA)
            pe.wait_ge(s_init, 3)
            pe.wait_ge(sems[MLA]["v"].sem, sems[MLA]["v"].at(B - 1))
            pe.transpose(B0[0:SC, 320:320 + B], mask_f[:], id32[0:B, 0:B])
            pe.transpose(B0[:, 256:256 + E], w_rt[:], id32[0:E, 0:E]).then_inc(s_small, 1)
            pe.wait_ge(s_prep2, 1)
            for k in (SA, CA):
                seam(pe, pe_step, k)
                warm_up(pe, k)
                steady(pe, pe_step, k)
            seam(pe, pe_step, CA + 1)
            pe.wait_ge(sems[CA]["done"].sem, sems[CA]["done"].at(B))
            pipeline(pe, mlp_pe_step, 1, 2)
            pe.wait_ge(f["l"].sem, f["l"].at(NQ))
            pipeline(pe, moe_pe_step, 1, 0)

        @block.scalar
        def _(act):
            act.wait_ge(s_prep, 1)
            seam(act, act_step, MLA)
            steady(act, act_step, MLA)
            act.wait_ge(s_prep2, 1)
            for k in (SA, CA):
                seam(act, act_step, k)
                if k == SA:
                    act.activation(mask_terms[:].rearrange("p b t -> p (b t)"),
                                   mask_rows[:].rearrange("p b t -> p (b t)"),
                                   ACT.Copy, scale=MASKED).then_inc(s_mr, 1)
                steady(act, act_step, k)
            seam(act, act_step, CA + 1)
            act.wait_ge(sems[CA]["done"].sem, sems[CA]["done"].at(B))
            pipeline(act, mlp_act_step, 1, 2)
            act.wait_ge(f["l"].sem, f["l"].at(NQ))
            pipeline(act, moe_act_step, 1, 0)

        @block.gpsimd
        def _(po):
            for signal in (*attn_sem.values(), *(x.sem for x in f.values()), *(x.sem for x in e.values())):
                po.sem_inc(signal, LEAD)
            po.wait_ge(s_prep, 1)
            seam(po, pool_step, MLA)
            steady(po, pool_step, MLA)
            for k in (SA, CA):
                seam(po, pool_step, k)
                steady(po, pool_step, k)
                if k == SA:
                    po.wait_ge(s_mr, 1)
            seam(po, pool_step, CA + 1)
            po.wait_ge(sems[CA]["done"].sem, sems[CA]["done"].at(B))
            pipeline(po, mlp_pool_step, 1, 2)
            po.wait_ge(f["l"].sem, f["l"].at(NQ))
            pipeline(po, moe_pool_step, 1, 0)

        @block.sync
        def _(sp):
            xv = a["x"].rearrange("b t d -> t b d")
            sp.dma_start(X[:, 0:4, :], xv[:, 0:4, :]).then_inc(s_x0, 16)
            for dst, name in ((id32[:], "c_ident"), (cosT[:], "c_cos"), (nsin[:], "c_nsin"),
                              (psin[:], "c_psin"), (causal[:], "c_causal"), (sel32[:], "c_sel")):
                sp.dma_start(dst, a[name]).then_inc(s_c, 16)
            sp.dma_start(w_dqkv[:, 0:DL], a["L0_attn_W_DQ"]).then_inc(s_w, 16)
            sp.dma_start(w_dqkv[:, DL:2 * DL], a["L0_attn_W_DKV"]).then_inc(s_w, 16)
            sp.dma_start(w_uq[:, 0:H * DH], a["L0_attn_W_UQ"]).then_inc(s_w, 16)
            sp.dma_start(w_uq[:, H * DH:], a["L0_attn_W_QR"]).then_inc(s_w, 16)
            sp.dma_start(w_ukv[:, 0:H * DH], a["L0_attn_W_UK"]).then_inc(s_w, 16)
            sp.dma_start(w_ukv[:, H * DH:], a["L0_attn_W_UV"]).then_inc(s_w, 16)
            sp.dma_start(w_mla[:, MEND - DR:MEND], a["L0_attn_W_KR"]).then_inc(s_w, 16)
            sp.dma_start(w_o[:, 0, :], a["L0_attn_W_O"]).then_inc(s_w, 16)
            for b0 in range(4, B, 20):
                sp.dma_start(X[:, b0:b0 + 20, :], xv[:, b0:b0 + 20, :]).then_inc(s_x1, 16)
            for k, name in enumerate(("q1W", "w1W", "q2W", "w2W")):
                sp.dma_start(w_raw[:, k, :], a["L0_xattn_" + name]).then_inc(s_w2, 16)
            sp.dma_start(w_o[:, 1, :], a["L0_xattn_o1W"]).then_inc(s_w2, 16)
            sp.dma_start(w_o[:, 2, :], a["L0_xattn_o2W"]).then_inc(s_w2, 16)
            sp.dma_start(w_f1[:], a["L0_xattn_ffW1"]).then_inc(s_w2, 16)
            sp.dma_start(w_f2[:], a["L0_xattn_ffW2"].rearrange("(c p) n -> p c n", p=128)).then_inc(s_w2, 16)
            sp.dma_start(b_f1[:], a["L0_xattn_ffb1"].rearrange("(c p) -> p c", p=128),
                         allow_slow_non_contiguous=True).then_inc(s_w2, 16)
            sp.dma_start(b_f2[:], a["L0_xattn_ffb2"].rearrange("(p o) -> p o", o=1)).then_inc(s_w2, 16)
            for k, name in enumerate(("g1", "b1", "g2", "b2", "g3", "b3")):
                sp.dma_start(gb[:, k, :], a["L0_xattn_" + name].partition_broadcast(128)).then_inc(s_w2, 16)
            sp.dma_start(w_rt[:], a["L0_ffn_router_w"]).then_inc(s_w2, 16)
            sp.dma_start(b_r[:], a["L0_ffn_router_b"].partition_broadcast(128)).then_inc(s_w2, 16)
            sp.dma_start(w_e[:], a["L0_ffn_expert_w"].rearrange("e h n -> h e n")).then_inc(s_w2, 16)
            sp.dma_start(mask_rows[:], a["mask_Bx1xS2x1_bk0"].rearrange("b o s p -> (b o) (s p)")
                         .partition_broadcast(128)).then_inc(s_m, 16)
            sp.dma_start(mask_b[:], a["mask_Bx1xS2x1_bk0"].rearrange("b o s p -> b (o s p)")).then_inc(s_m, 16)

            s = sems[CA]

            for i in range(2):
                sp.dma_start(cx[:, i, :], a["ctx_1024"][i]).then_inc(s_ctx[i], 16)
            with sp.Fori(1, B // 2) as t:
                for p in range(2):
                    sp.wait_ge(s["xnT_ps"].sem, s["xnT_ps"].at(2 * t + p - 1))
                    sp.dma_start(cx[:, p, :],
                                 a["ctx_1024"][bass.ds(2 * t + p, 1)].rearrange("o s d -> (o s) d")
                                 ).then_inc(s_ctx[p], 16)
            moe_store(sp)


_INS = ["x", "ctx_1024", "mask_Bx1xS2x1_bk0", "L0_attn_W_DQ", "L0_attn_W_UQ", "L0_attn_W_QR", "L0_attn_W_DKV",
        "L0_attn_W_UK", "L0_attn_W_UV", "L0_attn_W_KR", "L0_attn_W_O", "L0_xattn_q1W", "L0_xattn_w1W",
        "L0_xattn_o1W", "L0_xattn_q2W", "L0_xattn_w2W", "L0_xattn_o2W", "L0_xattn_ffW1", "L0_xattn_ffb1",
        "L0_xattn_ffW2", "L0_xattn_ffb2", "L0_xattn_g1", "L0_xattn_b1", "L0_xattn_g2", "L0_xattn_b2",
        "L0_xattn_g3", "L0_xattn_b3", "L0_ffn_router_w", "L0_ffn_router_b", "L0_ffn_expert_w"]


def shape_constants():
    f32 = np.float32
    ang = np.arange(S, dtype=f32)[:, None] * (f32(10000.0) ** (-np.arange(0, DR, 2, dtype=f32) / f32(DR)))
    ang = ang.astype(f32)
    key, query = np.arange(S)[:, None], np.arange(S)[None, :]
    part = np.arange(128)
    return {
        "c_ident": np.eye(128, dtype=f32),
        "c_cos": np.repeat(np.cos(ang), 2, axis=1).astype(f32),
        "c_nsin": (-np.sin(ang)).astype(f32),
        "c_psin": np.sin(ang).astype(f32),
        "c_causal": np.where(query >= key, math.exp(CLIP * SCALE_MLA), 0.0).astype(f32),
        "c_sel": (part[:, None] % 32 == np.arange(NG)[None, :]).astype(f32),
    }


def kernel(**inputs):
    import concourse.bacc as _bacc
    from concourse.bass_utils import run_bass_kernel_spmd as _run

    nc = _bacc.Bacc("TRN2", target_bir_lowering=False, num_devices=1)
    arrays, args = {}, {}
    given = {n: np.ascontiguousarray(inputs[n]) for n in _INS}
    for name, arr in {**given, **shape_constants()}.items():
        arrays[f"in_{name}"] = arr
        args[name] = nc.dram_tensor(f"in_{name}", arr.shape, mybir.dt.from_np(arr.dtype), kind="ExternalInput").ap()
    out = nc.dram_tensor("out_0_dram", (B, S, D), F32, kind="ExternalOutput").ap()
    decoder_kernel(nc, args, out)
    r = _run(nc, [arrays], core_ids=[0])
    return r.results[0]["out_0_dram"]
```

```python
import math
from contextlib import ExitStack

import numpy as np
import concourse.bass as bass
from concourse import mybir

F32 = mybir.dt.float32
F16 = mybir.dt.float16
BF16 = mybir.dt.bfloat16
U8 = mybir.dt.uint8
ALU = mybir.AluOpType
ACT = mybir.ActivationFunctionType
AX = mybir.AxisListType.X

B, S, D = 64, 128, 128
SC = 120
H, DH, DR, DL = 16, 8, 4, 32
FF = 4 * D
E, TOPK = 16, 6
NJ, NG = 4, H // 4
QW = 4
NQ = B // QW
LN_EPS = 1e-5
MOE_EPS = 1e-10
CLIP = 80.0
MASKED = -998244352.0
SCALE_MLA = 1.0 / math.sqrt(DH + DR)
SCALE_X = 1.0 / math.sqrt(DH)
P_LO = math.exp(-CLIP * SCALE_MLA)
MQ, MK, MV, MR = 0, H * DH, 2 * H * DH, 3 * H * DH
MEND = MR + H * DR + DR
ROWS_MLA = 2 * (DH + DR)
MLA, SA, CA = 0, 1, 2


LEAD = 16


FILL = (1, 4, 5)
FILL_END = (2, 0, 0)


class Signal:

    def __init__(self, sem, base=0):
        self.sem, self.base = sem, LEAD + base

    def at(self, n):
        return self.base + n


def apart(eng):
    eng.nop(nofuse=True)


def decoder_kernel(nc, a, out):
    ctx = ExitStack()
    with ctx:
        def sb(name, shape, dt=F32):
            return ctx.enter_context(nc.sbuf_tensor(name, shape, dt))

        def ps(name, shape, dt=F32):
            return ctx.enter_context(nc.psum_tensor(name, shape, dt))

        def sem(name):
            return ctx.enter_context(nc.semaphore(name))

        X = sb("X", [128, B, D])
        Y = sb("Y", [128, B, D])
        T = sb("T", [128, B, 128])
        L = sb("L", [128, B, E])
        id32 = sb("id32", [128, 128])
        id16 = sb("id16", [128, 128], F16)
        idb = sb("idb", [128, 128], BF16)
        cosT = sb("cosT", [128, DR])
        nsin = sb("nsin", [128, DR // 2])
        psin = sb("psin", [128, DR // 2])
        causal = sb("causal", [128, 128])
        sel32 = sb("sel32", [128, H])
        sel = sb("sel", [128, H, 128], BF16)
        mean = sb("mean", [128, 128], BF16)
        neghalf = sb("neghalf", [128, 4])
        w_dqkv = sb("w_dqkv", [128, 2 * DL])
        w_dT = sb("w_dT", [DL, 2, 128])
        w_uq = sb("w_uq", [DL, H * DH + H * DR])
        w_ukv = sb("w_ukv", [DL, 2 * H * DH])
        w_mla = sb("w_mla", [128, MEND])
        w_raw = sb("w_raw", [128, 4, D])
        w_x1 = sb("w_x1", [128, 2, D])
        w_x2 = sb("w_x2", [128, 2, D])
        w_o = sb("w_o", [128, 3, D])
        w_f1 = sb("w_f1", [128, FF])
        w_f2 = sb("w_f2", [128, FF // 128, D])
        b_f1 = sb("b_f1", [128, FF // 128])
        b_f2 = sb("b_f2", [128, 1])
        gb = sb("gb", [128, 6, D])
        w_rt = sb("w_rt", [E, D])
        w_r = sb("w_r", [128, E])
        b_r = sb("b_r", [128, E])
        w_e = sb("w_e", [128, E, D])
        mask_rows = sb("mask_rows", [128, B, SC], U8)
        mask_b = sb("mask_b", [B, SC], U8)
        mask_f = sb("mask_f", [B, SC])
        keep = sb("keep", [SC, B])
        maskbias = sb("maskbias", [SC, B])
        mask_terms = T[:].rearrange("p b t -> p (b t)")[:, 0:B * SC // 2].bitcast(BF16).rearrange(
            "p (b t) -> p b t", b=B)
        st6 = sb("st6", [128, 2, 6])
        mv = sb("mv", [128, 2, 2])
        veps = sb("veps", [128, 2])
        rstd = sb("rstd", [128, 2])
        xn = sb("xn", [128, 2, D])
        cx = sb("cx", [SC, 2, D])
        xnT = sb("xnT", [128, 2, 256])
        kf = sb("kf", [128, 2, H * DH])
        rt1 = sb("rt1", [128, 2, H + 1, DR])
        rt2 = sb("rt2", [128, 2, H + 1, DR])
        rr = sb("rr", [128, 2, H + 1, DR])
        QK = sb("QK", [128, 2, 3, H, 32], F16)
        QKT = sb("QKT", [128, 2, 3, NG, 128], F16)
        V = sb("V", [128, 2, H, 32])
        negm = sb("negm", [128, 2, NJ, 32], BF16)
        mT = sb("mT", [128, 2, 128], BF16)
        nmr = sb("nmr", [128, 2, SC], BF16)
        P = sb("P", [128, 2, NJ, NG, 128])
        OT = sb("OT", [128, 2, NG * 128])
        rden = sb("rden", [128, 2, H])
        O = sb("O", [128, 2, D])
        OTT = sb("OTT", [128, 2, 128])
        st6c = sb("st6c", [128, 2, 6])
        mvc = sb("mvc", [128, 2, 2])
        vepsc = sb("vepsc", [128, 2])
        rstdc = sb("rstdc", [128, 2])
        r0 = sb("r0", [128, 2, D])
        r1 = sb("r1", [128, 2, D])
        r2 = sb("r2", [128, 2, D])

        SS = ps("SS", [128, NJ, NG, 128])
        B0 = ps("B0", [128, 512])
        B1 = ps("B1", [128, 2, NG, 128], F16)
        B2 = ps("B2", [128, 512])
        B3 = ps("B3", [128, 512])
        B1f = B1[:].rearrange("r t g k -> r (t g k)").bitcast(F32)
        B3b = B3[:, 256:320].bitcast(BF16)
        B3k = B3[:, 128:384].bitcast(F16)

        s_x0, s_x1 = sem("x_first"), sem("x_rest")
        s_c, s_w, s_w2, s_m = (sem(n) for n in
                               ("consts_loaded", "mla_weights_loaded", "weights_loaded", "mask_loaded"))
        s_init, s_small = sem("init_done"), sem("small_transposed")
        s_wt, s_wtc, s_wf, s_wfc = (sem(n) for n in
                                    ("wd_transposed", "wd_copied", "wf_product", "wf_copied"))
        s_mr, s_prep2, s_prep = sem("mask_terms"), sem("later_weights_ready"), sem("weights_ready")
        per_batch = {
            "stats": (1, 1, 0), "aggr": (1, 1, 0), "veps": (1, 1, 0), "rstd": (1, 1, 0), "xn": (1, 1, 1),
            "xnT_ps": (1, 1, 1), "xnT": (1, 1, 1), "proj": (1, 1, 1), "v": (1, 1, 1), "kf": (0, 0, 1),
            "hi": (1, 2, 2), "lo": (1, 1, 1), "t1": (1, 0, 0), "rot": (1, 0, 0), "rhi": (1, 0, 0),
            "kb": (1, 0, 0), "kbT_ps": (1, 0, 0), "kbT": (1, 0, 0), "qkT_ps": (1, 1, 1), "qkT": (1, 1, 1), "nm": (0, 1, 1),
            "S": (0, 2, 2), "max": (0, 2, 2), "mT_ps": (0, 1, 1), "mT": (0, 1, 1), "ST": (2, 2, 2),
            "exp": (2, 2, 2), "clip": (4, 0, 0), "PV": (1, 1, 1), "OT": (1, 1, 1), "OTt": (1, 1, 1),
            "rden": (1, 1, 1), "O": (1, 1, 1), "O_ps": (1, 1, 1), "OTT": (1, 1, 1), "wo": (1, 1, 1),
            "took": (1, 1, 1), "statsc": (0, 1, 1), "aggrc": (0, 1, 1), "vepsc": (0, 1, 1),
            "rstdc": (0, 1, 1), "nrm": (0, 1, 1), "gain": (0, 1, 1), "done": (0, 1, 1)}
        attn_sem = {n: sem(f"attn_{n}") for n in per_batch}
        sems = [{n: Signal(attn_sem[n], B * sum(c[:k])) for n, c in per_batch.items()} for k in range(3)]
        s_ctx = [sem("ctx_loaded0"), sem("ctx_loaded1")]

        NW2 = 4 + 2 + 4 + 6 + 3

        block = ctx.enter_context(nc.Block())


        def pe_step(pe, p, norm, proj, soft, vals, outp):
            q = 1 - p

            def output(k, s):
                m = sems[k]
                pe.wait_ge(m["OTT"].sem, m["OTT"].at(s - 1))
                if soft:
                    pe.wait_ge(sems[soft[0]]["qkT"].sem, sems[soft[0]]["qkT"].at(soft[1] + 1))
                pe.matmul(B1f[:, 0:128], OTT[:, p, :], w_o[:, k, :], start=True, stop=True
                          ).then_inc(m["wo"].sem, 1)

            def project(k, s):
                m, nk = sems[k], SC if k == CA else S
                pe.wait_ge(m["xnT"].sem, m["xnT"].at(s + 2))
                pe.wait_ge(m["v"].sem, m["v"].at(s + 1))
                if k == MLA:
                    pe.matmul(B0[:, 0:MEND], xnT[:, q, 0:128], w_mla[:], start=True, stop=True
                              ).then_inc(m["proj"].sem, 1)
                elif k == SA:
                    pe.matmul(B0[:, 0:256], xnT[:, q, 0:128], w_x1[:].rearrange("p a n -> p (a n)"),
                              start=True, stop=True).then_inc(m["proj"].sem, 1)
                else:
                    pe.matmul(B0[:, 0:128], xnT[:, q, 0:128], w_x2[:, 0, :], start=True, stop=True)
                    pe.matmul(B0[0:nk, 128:256], xnT[:, q, 128:128 + nk], w_x2[:, 1, :],
                              start=True, stop=True).then_inc(m["proj"].sem, 1)

            def values_up(k, s):
                m = sems[k]
                pe.wait_ge(m["O"].sem, m["O"].at(s - 1))
                if not proj:
                    pe.wait_ge(m["OTT"].sem, m["OTT"].at(s - 2))
                    pe.wait_ge(m["mT"].sem, m["mT"].at(B if not soft else s))
                    pe.wait_ge(m["xnT"].sem, m["xnT"].at(B))
                pe.transpose(B3[:, 384:512], O[:, p, :], id32[:]).then_inc(m["O_ps"].sem, 1)

            def values(k, s, u):
                m, nk = sems[k], SC if k == CA else S
                done = m["clip"] if k == MLA else m["exp"]
                if u == 0:
                    pe.wait_ge(m["v"].sem, m["v"].at(s))
                    pe.wait_ge(m["O"].sem, m["O"].at(s - 1))
                pe.wait_ge(done.sem, done.at(4 * s + 2 * u - 2 if k == MLA else 2 * s + u - 1))
                for g in range(NG):
                    for j in (2 * u, 2 * u + 1):
                        mm = pe.matmul(B2[32 * j:32 * j + 32, g * 128:(g + 1) * 128],
                                       V[0:nk, q, 4 * g + j, :], P[0:nk, q, j, g, :],
                                       start=True, stop=True)
                if u == 1:
                    mm.then_inc(m["PV"].sem, 1)

            def scores(k, s, u):
                m, nk = sems[k], SC if k == CA else S
                if k == MLA:
                    if u == 0:
                        pe.wait_ge(m["qkT"].sem, m["qkT"].at(s + 1))
                        pe.wait_ge(m["kbT"].sem, m["kbT"].at(s + 1))
                    pe.wait_ge(m["exp"].sem, m["exp"].at(2 * s + u - 1))
                elif u == 0:
                    pe.wait_ge(m["mT"].sem, m["mT"].at(s + 1))
                for g in range(NG):
                    for j in (2 * u, 2 * u + 1):
                        if k == MLA:
                            r = slice(32 * j, 32 * j + ROWS_MLA)
                            pe.matmul(SS[:, j, g, :], QKT[r, p, 1, g, :], QKT[r, p, 0, g, :],
                                      start=True, stop=False)
                            mm = pe.matmul(SS[:, j, g, :], QKT[r, p, 2, g, :], QKT[r, p, 0, g, :],
                                           start=False, stop=True)
                        else:
                            r = slice(32 * j, 32 * j + 32)
                            pe.matmul(SS[0:nk, j, g, :], sel[:, 4 * g + j, 0:nk],
                                      mT[:, p, :], start=True, stop=False)
                            mm = pe.matmul(SS[0:nk, j, g, :], QKT[r, p, 1, g, 0:nk], QKT[r, p, 0, g, :],
                                           start=False, stop=True)
                mm.then_inc(m["ST"].sem, 1)

            if proj:
                k, s = proj
                m, nk = sems[k], SC if k == CA else S
                pe.wait_ge(m["xn"].sem, m["xn"].at(s + 2))
                pe.wait_ge(m["xnT"].sem, m["xnT"].at(s + 1))
                if k == MLA:
                    pe.wait_ge(m["kbT"].sem, m["kbT"].at(s + 1))
                if k == SA and isinstance(s, int):
                    pe.wait_ge(sems[MLA]["kbT"].sem, sems[MLA]["kbT"].at(B))
                if k != MLA:
                    pe.wait_ge(m["mT"].sem, m["mT"].at(s))
                pe.wait_ge(m["OTT"].sem, m["OTT"].at(s - 2))
                if k == CA:
                    pe.wait_ge(s_ctx[q], 8 * (s + 1 - q) + 16)
                    pe.transpose(B3[:, 128:128 + nk], cx[:, q, :], id32[0:nk, 0:nk])
                pe.transpose(B3[:, 0:128], xn[:, q, :], id32[:]).then_inc(m["xnT_ps"].sem, 1)
            late = bool(soft and soft[0] == MLA)
            if outp and not late:
                values_up(*outp)
            if soft and soft[0] != MLA:
                k, s = soft
                m, nk = sems[k], SC if k == CA else S
                pe.wait_ge(m["qkT"].sem, m["qkT"].at(s + 1))
                if k == SA and isinstance(s, int):
                    pe.wait_ge(sems[MLA]["exp"].sem, sems[MLA]["exp"].at(2 * B))
                if k == CA:
                    pe.wait_ge(m["nm"].sem, m["nm"].at(s + 1))
                for u in range(2):
                    pe.wait_ge(m["exp"].sem, m["exp"].at(2 * s + u - 1))
                    if k == CA:
                        for j in (2 * u, 2 * u + 1):
                            pe.matmul(SS[:, j, :, 0:nk], mean[:],
                                      nmr[:, p, :].unsqueeze(1).broadcast_to([128, NG, nk]),
                                      start=True, stop=False)
                    for g in range(NG):
                        for j in (2 * u, 2 * u + 1):
                            r = slice(32 * j, 32 * j + 32)
                            mm = pe.matmul(SS[:, j, g, 0:nk], QKT[r, p, 0, g, :], QKT[r, p, 1, g, 0:nk],
                                           start=(k != CA), stop=(k != CA or g == NG - 1))
                    mm.then_inc(m["S"].sem, 1)
                    if u == 0 and vals:
                        values(*vals, 0)
                    if u == 0 and outp:
                        output(*outp)
            else:
                if soft:
                    scores(*soft, 0)
                    if proj:
                        project(*proj)
                if outp and late:
                    values_up(*outp)
                if vals:
                    values(*vals, 0)
                if outp:
                    output(*outp)
            if proj and not (soft and soft[0] == MLA):
                project(*proj)
            if soft and soft[0] == MLA:
                scores(*soft, 1)
            if vals:
                values(*vals, 1)
            if proj and soft and outp:
                for _ in range(FILL[proj[0]]):
                    pe.matmul(B3[:], id16[:], id16[:].unsqueeze(1).broadcast_to([128, 4, 128]),
                              start=True, stop=True)
            if soft and soft[0] != MLA:
                k, s = soft
                m = sems[k]
                pe.wait_ge(m["max"].sem, m["max"].at(2 * s + 2))
                pe.wait_ge(m["xnT"].sem, m["xnT"].at(s + 2 if proj and proj[0] == k else B))
                if outp:
                    pe.wait_ge(sems[outp[0]]["OTT"].sem, sems[outp[0]]["OTT"].at(outp[1] - 1))
                pe.transpose(B3b, negm[:, p].rearrange("t j r -> t (j r)"), idb[:]).then_inc(m["mT_ps"].sem, 1)
            if proj:
                k, s = proj
                m, nk = sems[k], SC if k == CA else S
                pe.wait_ge(m["lo"].sem, m["lo"].at(s + 2))
                if outp:
                    pe.wait_ge(sems[outp[0]]["took"].sem, sems[outp[0]]["took"].at(outp[1] - 1))
                for t in range(2):
                    n = 128 if t == 0 else nk
                    for g in range(NG):
                        mm = pe.transpose(B1[:, t, g, 0:n],
                                          QK[0:n, q, t, 4 * g:4 * g + 4, :].rearrange("t h r -> t (h r)"),
                                          id16[0:n, 0:n])
                mm.then_inc(m["qkT_ps"].sem, 1)
            if proj and proj[0] == MLA:
                k, s = proj
                m = sems[k]
                pe.wait_ge(m["kb"].sem, m["kb"].at(s + 2))
                if outp:
                    pe.wait_ge(m["OTT"].sem, m["OTT"].at(s - 1))
                for g in range(NG):
                    mm = pe.transpose(B3k[:, g * 128:(g + 1) * 128],
                                      QK[:, q, 2, 4 * g:4 * g + 4, :].rearrange("t h r -> t (h r)"), id16[:])
                mm.then_inc(m["kbT_ps"].sem, 1)
            if soft and soft[0] != MLA:
                scores(*soft, 0)
            if vals:
                k, s = vals
                m = sems[k]
                pe.wait_ge(m["OT"].sem, m["OT"].at(s))
                for g in range(NG):
                    mm = pe.transpose(B2[:, g * 128:(g + 1) * 128], OT[:, q, g * 128:(g + 1) * 128], id32[:])
                mm.then_inc(m["OTt"].sem, 1)
            if soft and soft[0] != MLA:
                scores(*soft, 1)
            if proj and soft and outp:
                k, s = proj
                pe.wait_ge(sems[k]["v"].sem, sems[k]["v"].at(s + 2))
                for _ in range(FILL_END[k]):
                    pe.matmul(B0[:], id16[:], id16[:].unsqueeze(1).broadcast_to([128, 4, 128]),
                              start=True, stop=True)

        def act_step(act, p, norm, proj, soft, vals, outp):
            q = 1 - p

            def exps(k, s, u):
                m, nk = sems[k], SC if k == CA else S
                act.wait_ge(m["ST"].sem, m["ST"].at(2 * s + u + 1))
                act.wait_ge(m["PV"].sem, m["PV"].at(s - 1))
                o = P[0:nk, p, 2 * u:2 * u + 2].rearrange("k j g q -> k (j g q)")
                src = SS[0:nk, 2 * u:2 * u + 2].rearrange("k j g q -> k (j g q)")
                if k == CA:
                    apart(act)
                    act.activation(o, src, ACT.Exp, bias=maskbias[:, bass.ds(s, 1)], scale=SCALE_X
                                   ).then_inc(m["exp"].sem, 1)
                else:
                    act.activation(o, src, ACT.Exp, scale=SCALE_MLA if k == MLA else SCALE_X
                                   ).then_inc(m["exp"].sem, 1)

            if proj:
                k, s = proj
                m, nk = sems[k], SC if k == CA else S
                act.wait_ge(m["xnT_ps"].sem, m["xnT_ps"].at(s + 2))
                if outp and not (soft and soft[0] == MLA):
                    act.wait_ge(sems[outp[0]]["O_ps"].sem, sems[outp[0]]["O_ps"].at(outp[1] - 1))
                act.wait_ge(m["proj"].sem, m["proj"].at(s))
                n = 128 + nk if k == CA else 128
                act.activation(xnT[:, q, 0:n], B3[:, 0:n], ACT.Copy).then_inc(m["xnT"].sem, 1)
            if outp and not (soft and soft[0] == MLA):
                k, s = outp
                m = sems[k]
                act.wait_ge(m["O_ps"].sem, m["O_ps"].at(s - 1))
                act.wait_ge(m["wo"].sem, m["wo"].at(s - 3))
                act.activation(OTT[:, p, :], B3[:, 384:512], ACT.Copy).then_inc(m["OTT"].sem, 1)
            if soft and soft[0] == MLA:
                exps(*soft, 0)
            if proj:
                k, s = proj
                m, nk = sems[k], SC if k == CA else S
                act.wait_ge(m["proj"].sem, m["proj"].at(s + 2))
                act.wait_ge(m["qkT_ps"].sem, m["qkT_ps"].at(s))
                if k == MLA:
                    act.wait_ge(m["kb"].sem, m["kb"].at(s))
                if k == MLA:
                    act.activation(QK[:, q, 0:2, :, 0:DH],
                                   B0[:, 0:MV].rearrange("t (a h d) -> t a h d", a=2, d=DH),
                                   ACT.Copy).then_inc(m["hi"].sem, 1)
                else:
                    qv = B0[:, 0:128].rearrange("t (h o d) -> t h o d", o=1, d=DH).broadcast_to([128, H, 2, DH])
                    act.activation(QK[:, q, 0, :, 0:2 * DH].rearrange("t h (r d) -> t h r d", r=2), qv,
                                   ACT.Copy).then_inc(m["hi"].sem, 1)
                    if k == CA:
                        act.wait_ge(m["lo"].sem, m["lo"].at(s))
                        apart(act)
                        act.activation(kf[0:nk, q, :], B0[0:nk, 128:256], ACT.Copy,
                                       scale=keep[:, bass.ds(s + 1, 1)]).then_inc(m["kf"].sem, 1)
                    if k == CA:
                        act.wait_ge(m["kf"].sem, m["kf"].at(s + 2))
                        src = kf[0:nk, q, :]
                    else:
                        src = B0[0:nk, 128:256]
                    act.activation(QK[0:nk, q, 1].rearrange("t h (r z d) -> t h r z d", r=2, z=2)[:, :, :, 0, :],
                                   src.rearrange("t (h o d) -> t h o d", o=1, d=DH).broadcast_to([nk, H, 2, DH]),
                                   ACT.Copy).then_inc(m["hi"].sem, 1)
            if outp and soft and soft[0] == MLA:
                k, s = outp
                m = sems[k]
                act.wait_ge(m["O_ps"].sem, m["O_ps"].at(s - 1))
                act.wait_ge(m["wo"].sem, m["wo"].at(s - 3))
                act.activation(OTT[:, p, :], B3[:, 384:512], ACT.Copy).then_inc(m["OTT"].sem, 1)
            if vals and not (proj and proj[0] == MLA):
                k, s = vals
                m = sems[k]
                act.wait_ge(m["PV"].sem, m["PV"].at(s))
                act.wait_ge(m["OTt"].sem, m["OTt"].at(s - 2))
                act.activation(OT[:, q, :], B2[:], ACT.Copy).then_inc(m["OT"].sem, 1)
            if proj and proj[0] == MLA:
                k, s = proj
                m = sems[k]
                act.wait_ge(m["kbT_ps"].sem, m["kbT_ps"].at(s))
                h = DH + DR
                act.wait_ge(m["rhi"].sem, m["rhi"].at(s + 2))
                act.activation(QK[:, q, 2, :, h:2 * h], QK[:, q, 1, :, 0:h], ACT.Copy)
                act.wait_ge(m["lo"].sem, m["lo"].at(s + 2))
                act.activation(QK[:, q, 2, :, 0:h], QK[:, q, 1, :, h:2 * h], ACT.Copy).then_inc(m["kb"].sem, 1)
            if vals and proj and proj[0] == MLA:
                k, s = vals
                m = sems[k]
                act.wait_ge(m["PV"].sem, m["PV"].at(s))
                act.wait_ge(m["OTt"].sem, m["OTt"].at(s - 2))
                act.activation(OT[:, q, :], B2[:], ACT.Copy).then_inc(m["OT"].sem, 1)
            if proj:
                k, s = proj
                m, nk = sems[k], SC if k == CA else S
                act.wait_ge(m["PV"].sem, m["PV"].at(s))
                act.wait_ge(m["lo"].sem, m["lo"].at(s + 2))
                x = B0[0:nk, MV:MR] if k == MLA else B0[0:nk, 128:256]
                act.activation(V[0:nk, q, :, 0:DH], x.rearrange("t (h d) -> t h d", d=DH),
                               ACT.Copy).then_inc(m["v"].sem, 1)
            if soft and soft[0] != MLA:
                for u in range(2):
                    exps(*soft, u)
            if proj and proj[0] == MLA:
                k, s = proj
                m = sems[k]
                act.wait_ge(m["kbT_ps"].sem, m["kbT_ps"].at(s + 2))
                act.wait_ge(m["ST"].sem, m["ST"].at(2 * s))
                act.activation(QKT[:, q, 2].rearrange("r g k -> r (g k)"), B3k, ACT.Copy).then_inc(m["kbT"].sem, 1)
            if soft and soft[0] == MLA:
                exps(*soft, 1)

        def dve_step(v, p, norm, proj, soft, vals, outp):
            q = 1 - p

            def clip(s, j):
                m = sems[MLA]
                v.wait_ge(m["exp"].sem, m["exp"].at(2 * s + j // 2 + 1))
                v.scalar_tensor_tensor(P[:, p, j], P[:, p, j], P_LO,
                                       causal[:].unsqueeze(1).broadcast_to([128, NG, 128]),
                                       ALU.max, ALU.min).then_inc(m["clip"].sem, 1)

            if soft and soft[0] != MLA:
                k, s = soft
                m, nk = sems[k], SC if k == CA else S
                u = 0
                v.wait_ge(m["S"].sem, m["S"].at(2 * s + u + 1))
                v.wait_ge(m["mT_ps"].sem, m["mT_ps"].at(s - 1))
                v.tensor_reduce(negm[:, p, 2 * u:2 * u + 2, 0:NG], SS[:, 2 * u:2 * u + 2, :, 0:nk],
                                AX, ALU.max, negate=True).then_inc(m["max"].sem, 1)
            if norm and norm[0] != CA:
                k, s = norm
                m = sems[k]
                if k == SA and isinstance(s, int):
                    v.wait_ge(sems[MLA]["took"].sem, sems[MLA]["took"].at(s + 3))
                v.wait_ge(m["aggr"].sem, m["aggr"].at(s + 1))
                apart(v)
                v.bn_stats(st6[:, p, :], X[:, s + 2, :]).then_inc(m["stats"].sem, 1)
            if soft and soft[0] != MLA:
                k, s = soft
                m, nk = sems[k], SC if k == CA else S
                u = 1
                v.wait_ge(m["S"].sem, m["S"].at(2 * s + u + 1))
                v.wait_ge(m["mT_ps"].sem, m["mT_ps"].at(s - 1))
                v.tensor_reduce(negm[:, p, 2 * u:2 * u + 2, 0:NG], SS[:, 2 * u:2 * u + 2, :, 0:nk],
                                AX, ALU.max, negate=True).then_inc(m["max"].sem, 1)
            if norm and norm[0] != CA:
                k, s = norm
                m = sems[k]
                v.wait_ge(m["stats"].sem, m["stats"].at(s + 3))
                v.wait_ge(m["xn"].sem, m["xn"].at(s + 1))
                apart(v)
                v.bn_aggr(mv[:, p, :], st6[:, p, :]).then_inc(m["aggr"].sem, 1)
            if outp and outp[0] != MLA:
                k, s = outp
                m, i = sems[k], s - 2
                v.wait_ge(m["wo"].sem, m["wo"].at(s - 1))
                v.wait_ge(m["nrm"].sem, m["nrm"].at(s - 3))
                if k == SA:
                    v.wait_ge(m["nm"].sem, m["nm"].at(s - 1))
                v.tensor_tensor(r0[:, p, :], B1f[:, 0:128], Y[:, i, :], ALU.add).then_inc(m["took"].sem, 1)
            if proj:
                k, s = proj
                m, nk = sems[k], SC if k == CA else S
                v.wait_ge(m["hi"].sem, m["hi"].at((1 if k == MLA else 2) * (s + 2)))
                if k == MLA:
                    x = B0[:, MR:MEND].rearrange("t (h d) -> t h d", d=DR)
                    x2 = B0[:, MR:MEND].rearrange("t (h c e) -> t h c e", e=2, c=DR // 2)
                    y2 = rt2[:, q].rearrange("t h (c e) -> t h c e", e=2)
                    n = [128, H + 1, DR // 2]
                    v.wait_ge(m["rot"].sem, m["rot"].at(s))
                    v.tensor_tensor(rt1[:, q], x, cosT[:].unsqueeze(1).broadcast_to([128, H + 1, DR]), ALU.mult)
                    v.tensor_tensor(y2[:, :, :, 0], x2[:, :, :, 1], nsin[:].unsqueeze(1).broadcast_to(n), ALU.mult)
                    v.tensor_tensor(y2[:, :, :, 1], x2[:, :, :, 0], psin[:].unsqueeze(1).broadcast_to(n),
                                    ALU.mult).then_inc(m["t1"].sem, 1)
                    v.tensor_tensor(QK[:, q, 0:2, :, DH + DR:2 * DH + DR],
                                    B0[:, 0:MV].rearrange("t (a h d) -> t a h d", a=2, d=DH),
                                    QK[:, q, 0:2, :, 0:DH], ALU.subtract)
                    v.wait_ge(m["t1"].sem, m["t1"].at(s + 2))
                    v.wait_ge(m["lo"].sem, m["lo"].at(s))
                    v.tensor_tensor(rr[:, q], rt1[:, q], rt2[:, q], ALU.add).then_inc(m["rot"].sem, 1)
                    v.wait_ge(m["rot"].sem, m["rot"].at(s + 2))
                    qr = rr[:, q, 0:H, :]
                    kr = rr[:, q, H:H + 1, :].broadcast_to([128, H, DR])
                    v.tensor_copy(QK[:, q, 0, :, DH:DH + DR], qr)
                    v.tensor_copy(QK[:, q, 1, :, DH:DH + DR], kr).then_inc(m["rhi"].sem, 1)
                    v.wait_ge(m["rhi"].sem, m["rhi"].at(s + 2))
                    v.tensor_tensor(QK[:, q, 0, :, 2 * DH + DR:ROWS_MLA], qr, QK[:, q, 0, :, DH:DH + DR],
                                    ALU.subtract)
                    v.tensor_tensor(QK[:, q, 1, :, 2 * DH + DR:ROWS_MLA], kr, QK[:, q, 1, :, DH:DH + DR],
                                    ALU.subtract).then_inc(m["lo"].sem, 1)
                else:
                    ksrc = kf[0:nk, q, :] if k == CA else B0[0:nk, 128:256]
                    bc = lambda z, n: z.rearrange("t (h o d) -> t h o d", o=1, d=DH).broadcast_to([n, H, 2, DH])
                    v.tensor_tensor(QK[:, q, 0, :, 2 * DH:32].rearrange("t h (r d) -> t h r d", r=2),
                                    bc(B0[:, 0:128], 128),
                                    QK[:, q, 0, :, 0:2 * DH].rearrange("t h (r d) -> t h r d", r=2),
                                    ALU.subtract)
                    kv = QK[0:nk, q, 1].rearrange("t h (r z d) -> t h r z d", r=2, z=2)
                    v.tensor_tensor(kv[:, :, :, 1, :], bc(ksrc, nk), kv[:, :, :, 0, :],
                                    ALU.subtract).then_inc(m["lo"].sem, 1)
            if outp and outp[0] == MLA:
                k, s = outp
                m, i = sems[k], s - 2
                v.wait_ge(m["wo"].sem, m["wo"].at(s - 1))
                v.tensor_tensor(X[:, i, :], B1f[:, 0:128], X[:, i, :], ALU.add).then_inc(m["took"].sem, 1)
            if norm and norm[0] == MLA:
                k, s = norm
                m = sems[k]
                v.wait_ge(m["rstd"].sem, m["rstd"].at(s + 3))
                v.wait_ge(m["xnT_ps"].sem, m["xnT_ps"].at(s + 1))
                v.tensor_scalar(xn[:, p, :], X[:, s + 2, :], mv[:, p, 0:1], rstd[:, p:p + 1],
                                ALU.subtract, ALU.mult).then_inc(m["xn"].sem, 1)
            if soft and soft[0] == MLA:
                clip(soft[1], 0)
            if soft and soft[0] != MLA:
                k, s = soft
                m = sems[k]
                v.wait_ge(m["mT_ps"].sem, m["mT_ps"].at(s + 1))
                v.wait_ge(m["ST"].sem, m["ST"].at(2 * s - 2))
                v.tensor_copy(mT[:, p, :], B3b).then_inc(m["mT"].sem, 1)
            if outp and outp[0] != MLA:
                k, s = outp
                m = sems[k]
                v.wait_ge(m["took"].sem, m["took"].at(s - 1))
                v.wait_ge(m["aggrc"].sem, m["aggrc"].at(s - 3))
                apart(v)
                v.bn_stats(st6c[:, p, :], r0[:, p, :]).then_inc(m["statsc"].sem, 1)
            if proj:
                k, s = proj
                m, nk = sems[k], SC if k == CA else S
                v.wait_ge(m["qkT_ps"].sem, m["qkT_ps"].at(s + 2))
                v.wait_ge(m["ST"].sem, m["ST"].at(2 * s))
                if k == CA:
                    v.tensor_copy(QKT[:, q, 0].rearrange("r g k -> r (g k)"), B1[:, 0].rearrange("r g k -> r (g k)"))
                    v.tensor_copy(QKT[:, q, 1, :, 0:nk], B1[:, 1, :, 0:nk]).then_inc(m["qkT"].sem, 1)
                else:
                    v.tensor_copy(QKT[:, q, 0:2].rearrange("r t g k -> r (t g k)"),
                                  B1[:].rearrange("r t g k -> r (t g k)")).then_inc(m["qkT"].sem, 1)
            if outp and outp[0] != MLA:
                k, s = outp
                m = sems[k]
                v.wait_ge(m["statsc"].sem, m["statsc"].at(s - 1))
                v.wait_ge(m["nrm"].sem, m["nrm"].at(s - 3))
                apart(v)
                v.bn_aggr(mvc[:, p, :], st6c[:, p, :]).then_inc(m["aggrc"].sem, 1)
            if soft and soft[0] == MLA:
                clip(soft[1], 1)
            if norm and norm[0] == SA:
                k, s = norm
                m = sems[k]
                v.wait_ge(m["rstd"].sem, m["rstd"].at(s + 3))
                v.wait_ge(m["xnT_ps"].sem, m["xnT_ps"].at(s + 1))
                v.wait_ge(m["nm"].sem, m["nm"].at(s + 1))
                v.tensor_scalar(xn[:, p, :], X[:, s + 2, :], mv[:, p, 0:1], rstd[:, p:p + 1],
                                ALU.subtract, ALU.mult).then_inc(m["xn"].sem, 1)
            if vals:
                k, s = vals
                m = sems[k]
                v.wait_ge(m["OTt"].sem, m["OTt"].at(s))
                v.wait_ge(m["O"].sem, m["O"].at(s - 2))
                ot = B2[:].rearrange("t (h r) -> t h r", r=32)
                v.reciprocal(rden[:, q, :], ot[:, :, DH]).then_inc(m["rden"].sem, 1)
            if vals:
                k, s = vals
                m = sems[k]
                v.wait_ge(m["rden"].sem, m["rden"].at(s))
                v.wait_ge(m["O_ps"].sem, m["O_ps"].at(s - 2))
                o = (O[:, q, :].rearrange("t (h d) -> t h d", d=DH) if k == MLA
                     else O[:, q, :].rearrange("t (d h) -> t h d", d=DH))
                v.tensor_tensor(o, ot[:, :, 0:DH], rden[:, q, :].unsqueeze(2).broadcast_to([128, H, DH]),
                                ALU.mult).then_inc(m["O"].sem, 1)
            if outp and outp[0] != MLA:
                k, s = outp
                m = sems[k]
                v.wait_ge(m["rstdc"].sem, m["rstdc"].at(s - 1))
                v.wait_ge(m["gain"].sem, m["gain"].at(s - 3))
                v.tensor_scalar(r1[:, p, :], r0[:, p, :], mvc[:, p, 0:1], rstdc[:, p:p + 1],
                                ALU.subtract, ALU.mult).then_inc(m["nrm"].sem, 1)
            if outp and outp[0] != MLA:
                k, s = outp
                m = sems[k]
                v.wait_ge(m["nrm"].sem, m["nrm"].at(s - 1))
                v.wait_ge(m["done"].sem, m["done"].at(s - 3))
                v.tensor_tensor(r2[:, p, :], r1[:, p, :], gb[:, 2 * (k - 1), :], ALU.mult
                                ).then_inc(m["gain"].sem, 1)
            if outp and outp[0] != MLA:
                k, s = outp
                m = sems[k]
                v.wait_ge(m["gain"].sem, m["gain"].at(s - 1))
                v.tensor_tensor(Y[:, s - 2, :], r2[:, p, :], gb[:, 2 * (k - 1) + 1, :], ALU.add
                                ).then_inc(m["done"].sem, 1)
            if soft and soft[0] == MLA:
                clip(soft[1], 2)
                clip(soft[1], 3)

        def pool_step(po, p, norm, proj, soft, vals, outp):
            q = 1 - p
            if norm and norm[0] == CA:
                k, s = norm
                m = sems[k]
                if isinstance(s, int):
                    po.wait_ge(sems[SA]["done"].sem, sems[SA]["done"].at(s + 3))
                po.wait_ge(m["xnT_ps"].sem, m["xnT_ps"].at(s + 1))
                apart(po)
                po.tensor_copy(xn[:, p, :], Y[:, s + 2, :]).then_inc(m["xn"].sem, 1)
            if norm and norm[0] != CA:
                k, s = norm
                m = sems[k]
                po.wait_ge(m["aggr"].sem, m["aggr"].at(s + 3))
                po.wait_ge(m["rstd"].sem, m["rstd"].at(s + 1))
                apart(po)
                po.tensor_scalar(veps[:, p:p + 1], mv[:, p, 1:2], LN_EPS, None, ALU.add).then_inc(m["veps"].sem, 1)
                po.wait_ge(m["veps"].sem, m["veps"].at(s + 3))
                po.wait_ge(m["xn"].sem, m["xn"].at(s + 1))
                po.tensor_tensor(rstd[:, p:p + 1], veps[:, p:p + 1], neghalf[:, 1:2], ALU.pow
                                 ).then_inc(m["rstd"].sem, 1)
            if outp and outp[0] != MLA:
                k, s = outp
                m = sems[k]
                po.wait_ge(m["aggrc"].sem, m["aggrc"].at(s - 1))
                po.wait_ge(m["rstdc"].sem, m["rstdc"].at(s - 3))
                apart(po)
                po.tensor_scalar(vepsc[:, p:p + 1], mvc[:, p, 1:2], LN_EPS, None, ALU.add
                                 ).then_inc(m["vepsc"].sem, 1)
                po.wait_ge(m["vepsc"].sem, m["vepsc"].at(s - 1))
                po.wait_ge(m["nrm"].sem, m["nrm"].at(s - 3))
                po.tensor_tensor(rstdc[:, p:p + 1], vepsc[:, p:p + 1], neghalf[:, 1:2], ALU.pow
                                 ).then_inc(m["rstdc"].sem, 1)
            if norm and norm[0] == SA:
                k, s = norm
                m = sems[k]
                po.wait_ge(m["xn"].sem, m["xn"].at(s + 3))
                apart(po)
                po.tensor_copy(Y[:, s + 2, :], xn[:, p, :]).then_inc(m["nm"].sem, 1)
            if norm and norm[0] == CA:
                k, s = norm
                m = sems[k]
                po.wait_ge(m["S"].sem, m["S"].at(2 * (s + 1)))
                apart(po)
                po.tensor_copy(nmr[:, p, :], mask_terms[:, s + 2, :]).then_inc(m["nm"].sem, 1)

        def seam(eng, step, k):
            for s in range(-2, 2):
                pieces = []
                for ahead in (2, 1, 0, -1, -2):
                    kk = k if s + ahead >= 0 else k - 1
                    pieces.append((kk, s if kk == k else s + B) if 0 <= kk <= CA else None)
                step(eng, s % 2, *pieces)

        def steady(eng, step, k):
            with eng.Fori(1, B // 2 - 1) as t:
                for p in range(2):
                    at = (k, 2 * t + p)
                    step(eng, p, at, at, at, at, at)

        fn = ["y", "yT_ps", "yT", "h_ps", "h", "o_ps", "o", "b_ps", "r", "st", "ag", "ve", "rs", "n", "g",
              "f", "x2", "st2", "ag2", "ve2", "rs2", "n2", "t_ps", "t", "l_ps", "l"]
        f = {n: Signal(sem(f"mlp_{n}")) for n in fn}
        yb = sb("yb", [128, 2, QW, D])
        yT = sb("yT", [128, 2, QW * 128])
        hT = P[:].rearrange("p a j g q -> p a j (g q)")
        oT = OT
        rb = sb("rb", [128, QW, D])
        nb = sb("nb", [128, QW, D])
        t2 = sb("t2", [128, QW, D])
        st24 = sb("st24", [128, QW, 6])
        mv8 = sb("mv8", [128, QW, 2])
        ve4 = sb("ve4", [128, QW])
        rs4 = sb("rs4", [128, QW])
        st24b = sb("st24b", [128, QW, 6])
        mv8b = sb("mv8b", [128, QW, 2])
        ve4b = sb("ve4b", [128, QW])
        rs4b = sb("rs4b", [128, QW])
        NHC = FF // 128

        tT = QKT[:].rearrange("r a t g k -> r (a t g k)").bitcast(F32)[:, 0:2 * QW * 128].rearrange(
            "r (a n) -> r a n", a=2)

        def pipeline(eng, step, ahead, behind):
            head = -ahead
            first = behind + (behind + ahead) % 2 + (ahead % 2)
            first += first % 2
            last = (NQ - ahead) // 2 * 2
            for s in range(head, first):
                step(eng, s, s % 2, lambda d, s=s: 0 <= s + d < NQ)
            with eng.Fori(first // 2, last // 2) as t:
                for p in range(2):
                    step(eng, 2 * t + p, p, lambda d: True)
            for s in range(last, NQ + behind):
                step(eng, s, s % 2, lambda d, s=s: 0 <= s + d < NQ)


        def mlp_rstd(po, s, mv8, ve4, rs4, ag, ve, rs):
            po.wait_ge(f[ag].sem, f[ag].at(s))
            apart(po)
            po.tensor_scalar(ve4[:], mv8[:, :, 1], LN_EPS, None, ALU.add).then_inc(f[ve].sem, 1)
            po.wait_ge(f[ve].sem, f[ve].at(s))
            po.tensor_tensor(rs4[:], ve4[:], neghalf[:, 1:2].broadcast_to([128, QW]), ALU.pow
                             ).then_inc(f[rs].sem, 1)

        def mlp_pool_step(po, s, p, runs):
            if runs(-1):
                mlp_rstd(po, s, mv8, ve4, rs4, "ag", "ve", "rs")
            if runs(-2):
                mlp_rstd(po, s - 1, mv8b, ve4b, rs4b, "ag2", "ve2", "rs2")
            if runs(2):
                po.wait_ge(f["yT_ps"].sem, f["yT_ps"].at(s + 1))
                apart(po)
                po.tensor_copy(yb[:, p], Y[:, bass.ds(QW * (s + 2), QW), :]).then_inc(f["y"].sem, 1)

        def mlp_pe_step(pe, s, p, runs):
            q = 1 - p
            if runs(1):
                pe.wait_ge(f["y"].sem, f["y"].at(s + 2))
                pe.wait_ge(f["l"].sem, f["l"].at(s - 3))
                pe.wait_ge(f["yT"].sem, f["yT"].at(s + 1))
                for b in range(QW):
                    mm = pe.transpose(B0[:, b * 128:(b + 1) * 128], yb[:, q, b, :], id32[:])
                mm.then_inc(f["yT_ps"].sem, 1)
            if runs(-1):
                pe.wait_ge(f["o"].sem, f["o"].at(s))
                pe.wait_ge(f["r"].sem, f["r"].at(s - 1))
                for b in range(QW):
                    mm = pe.transpose(B3[:, b * 128:(b + 1) * 128], oT[:, q, b * 128:(b + 1) * 128], id32[:])
                mm.then_inc(f["b_ps"].sem, 1)
            for c in range(NHC):
                if runs(0):
                    if c == 0:
                        pe.wait_ge(f["yT"].sem, f["yT"].at(s + 1))
                    pe.wait_ge(f["h"].sem, f["h"].at(NHC * s - NHC + c + 1))
                    pe.matmul(SS[:, c].rearrange("p g q -> p (g q)"), w_f1[:, c * 128:(c + 1) * 128],
                              yT[:, p, :], start=True, stop=True).then_inc(f["h_ps"].sem, 1)
                if runs(-3) and c == 1:
                    pe.wait_ge(f["n2"].sem, f["n2"].at(s - 2))
                    pe.wait_ge(f["t"].sem, f["t"].at(s - 3))
                    for b in range(QW):
                        mm = pe.transpose(B1f[:, b * 128:(b + 1) * 128], t2[:, b, :], id32[:])
                    mm.then_inc(f["t_ps"].sem, 1)
            if runs(-3):
                pe.wait_ge(f["t"].sem, f["t"].at(s - 2))
                if runs(1):
                    pe.wait_ge(f["yT"].sem, f["yT"].at(s + 2))
                else:
                    pe.wait_ge(f["l"].sem, f["l"].at(s - 3))
                for b in range(QW):
                    mm = pe.matmul(B0[:, b * E:(b + 1) * E], tT[:, p, b * 128:(b + 1) * 128], w_r[:],
                                   start=True, stop=True)
                mm.then_inc(f["l_ps"].sem, 1)
            if runs(0):
                pe.wait_ge(f["o"].sem, f["o"].at(s))
                for c in range(NHC):
                    pe.wait_ge(f["h"].sem, f["h"].at(NHC * s + c + 1))
                    mm = pe.matmul(B2[:], w_f2[:, c, :], hT[:, p, c, :], start=(c == 0), stop=(c == NHC - 1))
                mm.then_inc(f["o_ps"].sem, 1)

        def mlp_act_step(act, s, p, runs):
            q = 1 - p
            if runs(1):
                act.wait_ge(f["yT_ps"].sem, f["yT_ps"].at(s + 2))
                act.wait_ge(f["h_ps"].sem, f["h_ps"].at(NHC * s))
                act.activation(yT[:, q, :], B0[:], ACT.Copy).then_inc(f["yT"].sem, 1)
            for c in range(NHC):
                if runs(0):
                    act.wait_ge(f["h_ps"].sem, f["h_ps"].at(NHC * s + c + 1))
                    act.wait_ge(f["o_ps"].sem, f["o_ps"].at(s - 1))
                    act.activation(hT[:, p, c, :], SS[:, c].rearrange("p g q -> p (g q)"), ACT.Gelu,
                                   bias=b_f1[:, c:c + 1]).then_inc(f["h"].sem, 1)
                if runs(-3) and c == 1:
                    act.wait_ge(f["t_ps"].sem, f["t_ps"].at(s - 2))
                    act.wait_ge(f["l_ps"].sem, f["l_ps"].at(s - 4))
                    act.activation(tT[:, p, :], B1f, ACT.Copy)
                    act.activation(T[:, bass.ds(QW * (s - 3), QW), :], B1f.rearrange("p (b t) -> p b t", b=QW),
                                   ACT.Copy).then_inc(f["t"].sem, 1)
            if runs(0):
                act.wait_ge(f["o_ps"].sem, f["o_ps"].at(s + 1))
                act.wait_ge(f["b_ps"].sem, f["b_ps"].at(s - 1))
                act.activation(oT[:, p, :], B2[:], ACT.Identity, bias=b_f2[:, 0:1]).then_inc(f["o"].sem, 1)

        def mlp_dve_step(v, s, p, runs):
            i = s - 1
            if runs(-1):
                v.wait_ge(f["b_ps"].sem, f["b_ps"].at(s))
                v.tensor_tensor(rb[:], B3[:].rearrange("t (b d) -> t b d", b=QW), Y[:, bass.ds(QW * i, QW), :],
                                ALU.add).then_inc(f["r"].sem, 1)
                v.wait_ge(f["r"].sem, f["r"].at(s))
                apart(v)
                for b in range(QW):
                    ins = v.bn_stats(st24[:, b, :], rb[:, b, :])
                ins.then_inc(f["st"].sem, 1)
                v.wait_ge(f["st"].sem, f["st"].at(s))
                apart(v)
                for b in range(QW):
                    ins = v.bn_aggr(mv8[:, b, :], st24[:, b, :])
                ins.then_inc(f["ag"].sem, 1)
            if runs(-2):
                v.wait_ge(f["x2"].sem, f["x2"].at(s - 1))
                apart(v)
                for b in range(QW):
                    ins = v.bn_stats(st24b[:, b, :], X[:, QW * (s - 2) + b, :])
                ins.then_inc(f["st2"].sem, 1)
                v.wait_ge(f["st2"].sem, f["st2"].at(s - 1))
                v.wait_ge(f["n2"].sem, f["n2"].at(s - 2))
                apart(v)
                for b in range(QW):
                    ins = v.bn_aggr(mv8b[:, b, :], st24b[:, b, :])
                ins.then_inc(f["ag2"].sem, 1)
            if runs(-1):
                v.wait_ge(f["rs"].sem, f["rs"].at(s))
                for b in range(QW):
                    ins = v.tensor_scalar(nb[:, b, :], rb[:, b, :], mv8[:, b, 0:1], rs4[:, b:b + 1],
                                          ALU.subtract, ALU.mult)
                ins.then_inc(f["n"].sem, 1)
                v.wait_ge(f["n"].sem, f["n"].at(s))
                v.tensor_tensor(rb[:], nb[:], gb[:, 4:5, :].broadcast_to([128, QW, D]), ALU.mult
                                ).then_inc(f["g"].sem, 1)
            if runs(-2):
                v.wait_ge(f["rs2"].sem, f["rs2"].at(s - 1))
                v.wait_ge(f["t_ps"].sem, f["t_ps"].at(s - 2))
                for b in range(QW):
                    ins = v.tensor_scalar(t2[:, b, :], X[:, QW * (s - 2) + b, :], mv8b[:, b, 0:1],
                                          rs4b[:, b:b + 1], ALU.subtract, ALU.mult)
                ins.then_inc(f["n2"].sem, 1)
            if runs(-1):
                v.wait_ge(f["g"].sem, f["g"].at(s))
                v.tensor_tensor(nb[:], rb[:], gb[:, 5:6, :].broadcast_to([128, QW, D]), ALU.add
                                ).then_inc(f["f"].sem, 1)
            if runs(-3):
                v.wait_ge(f["l_ps"].sem, f["l_ps"].at(s - 2))
                v.tensor_tensor(L[:, bass.ds(QW * (s - 3), QW), :],
                                B0[:, 0:QW * E].rearrange("t (b e) -> t b e", e=E),
                                b_r[:].unsqueeze(1).broadcast_to([128, QW, E]), ALU.add).then_inc(f["l"].sem, 1)
            if runs(-1):
                v.wait_ge(f["f"].sem, f["f"].at(s))
                xs = X[:, bass.ds(QW * i, QW), :]
                v.tensor_tensor(xs, xs, nb[:], ALU.add).then_inc(f["x2"].sem, 1)

        en = ["lm", "ld", "ex", "sm", "rc", "pr", "t8", "t8s", "mr", "sl", "gs", "s6", "s6e", "r6", "g1",
              "ga", "gm", "gr", "gate", "gp", "tb", "y", "acc", "sc", "p1", "p2", "p3", "ab", "out"]
        e = {n: Signal(sem(f"moe_{n}")) for n in en}
        e_st = [sem("moe_stored0"), sem("moe_stored1")]
        NA = 8
        ND = E - NA
        lm = sb("lm", [128, QW])
        le = sb("le", [128, QW, E])
        ssum = sb("ssum", [128, QW])
        p18 = sb("p18", [128, QW, E + 2])
        t8 = sb("t8", [128, QW, 8])
        mr = sb("mr", [128, QW, E + 2])
        gsel = sb("gsel", [128, QW, E])
        graw = sb("graw", [128, QW, E])
        g6 = sb("g6", [128, QW, 4])
        gate = sb("gate", [128, 2, QW, E])
        epsT = sb("epsT", [128, 2, QW])
        flat = P[:].rearrange("p a j g q -> p (a j g q)")
        n0, n1, n2 = 2 * QW * 128, 2 * NA * D, 2 * 4 * D
        tb = flat[:, 0:n0].rearrange("p (a b t) -> p a b t", a=2, b=QW)
        sc = flat[:, n0:n0 + n1].rearrange("p (a x d) -> p a x d", a=2, x=NA)
        padd = flat[:, n0 + n1:n0 + n1 + n2].rearrange("p (a x d) -> p a x d", a=2, x=4)
        acc = OT[:].rearrange("t a (x d) -> t a x d", d=D)[:, :, 0:2]
        psum3 = sb("psum3", [128, 2, D])
        ob = O


        def moe_logits(v, s):
            v.wait_ge(e["gate"].sem, e["gate"].at(s))
            ls = L[:, bass.ds(QW * s, QW), :]
            v.tensor_reduce(lm[:], ls, AX, ALU.max).then_inc(e["lm"].sem, 1)
            v.wait_ge(e["lm"].sem, e["lm"].at(s + 1))
            v.tensor_tensor(le[:], ls, bc(lm[:]), ALU.subtract).then_inc(e["ld"].sem, 1)

        def bc(z):
            return z.unsqueeze(2).broadcast_to([128, QW, E])

        NGATE = 16

        def gate_stage(v, n, s, p):
            if n == 0:
                v.wait_ge(e["ex"].sem, e["ex"].at(s + 1))
                v.tensor_reduce(ssum[:], le[:], AX, ALU.add).then_inc(e["sm"].sem, 1)
            elif n == 1:
                v.wait_ge(e["sm"].sem, e["sm"].at(s + 1))
                v.reciprocal(lm[:], ssum[:]).then_inc(e["rc"].sem, 1)
            elif n == 2:
                v.wait_ge(e["rc"].sem, e["rc"].at(s + 1))
                v.tensor_tensor(p18[:, :, 0:E], le[:], bc(lm[:]), ALU.mult).then_inc(e["pr"].sem, 1)
            elif n == 3:
                v.wait_ge(e["pr"].sem, e["pr"].at(s + 1))
                apart(v)
                for b in range(QW):
                    ins = v.max(t8[:, b, :], p18[:, b, 0:E])
                ins.then_inc(e["t8"].sem, 1)
            elif n == 4:
                v.wait_ge(e["t8"].sem, e["t8"].at(s + 1))
                v.memset(t8[:, :, TOPK:8], -1.0).then_inc(e["t8s"].sem, 1)
            elif n == 5:
                v.wait_ge(e["t8s"].sem, e["t8s"].at(s + 1))
                apart(v)
                for b in range(QW):
                    ins = v.match_replace(mr[:, b, :], t8[:, b, :], p18[:, b, :], -2.0)
                ins.then_inc(e["mr"].sem, 1)
            elif n == 6:
                v.wait_ge(e["mr"].sem, e["mr"].at(s + 1))
                v.tensor_scalar(gsel[:], mr[:, :, 0:E], -1.5, None, ALU.is_lt).then_inc(e["sl"].sem, 1)
            elif n == 7:
                v.wait_ge(e["sl"].sem, e["sl"].at(s + 1))
                v.tensor_tensor(graw[:], gsel[:], p18[:, :, 0:E], ALU.mult).then_inc(e["gs"].sem, 1)
            elif n == 8:
                v.wait_ge(e["gs"].sem, e["gs"].at(s + 1))
                v.tensor_reduce(g6[:, :, 0], graw[:], AX, ALU.add).then_inc(e["s6"].sem, 1)
            elif n == 9:
                v.wait_ge(e["s6"].sem, e["s6"].at(s + 1))
                v.tensor_scalar(g6[:, :, 1], g6[:, :, 0], MOE_EPS, None, ALU.add).then_inc(e["s6e"].sem, 1)
            elif n == 10:
                v.wait_ge(e["s6e"].sem, e["s6e"].at(s + 1))
                v.reciprocal(g6[:, :, 2], g6[:, :, 1]).then_inc(e["r6"].sem, 1)
            elif n == 11:
                v.wait_ge(e["r6"].sem, e["r6"].at(s + 1))
                v.tensor_tensor(gsel[:], graw[:], bc(g6[:, :, 2]), ALU.mult).then_inc(e["g1"].sem, 1)
            elif n == 12:
                v.wait_ge(e["g1"].sem, e["g1"].at(s + 1))
                v.tensor_reduce(g6[:, :, 3], gsel[:], AX, ALU.add).then_inc(e["ga"].sem, 1)
            elif n == 13:
                v.wait_ge(e["ga"].sem, e["ga"].at(s + 1))
                v.tensor_scalar(epsT[:, p], g6[:, :, 3], MOE_EPS, None, ALU.mult)
                v.tensor_scalar(g6[:, :, 0], g6[:, :, 3], MOE_EPS, None, ALU.max).then_inc(e["gm"].sem, 1)
            elif n == 14:
                v.wait_ge(e["gm"].sem, e["gm"].at(s + 1))
                v.reciprocal(g6[:, :, 1], g6[:, :, 0]).then_inc(e["gr"].sem, 1)
            elif n == 15:
                v.wait_ge(e["gr"].sem, e["gr"].at(s + 1))
                v.wait_ge(e["sc"].sem, e["sc"].at(QW * (s - 1)))
                v.tensor_tensor(gate[:, p], gsel[:], bc(g6[:, :, 1]), ALU.mult).then_inc(e["gate"].sem, 1)

        def bank(b2, c):
            if b2 == 0:
                return SS[:, c].rearrange("p g q -> p (g q)")
            return (B0[:], B1f, B2[:], B3[:])[c]

        def moe_pe_step(pe, s, p, runs):
            if not runs(0):
                return
            pe.wait_ge(e["tb"].sem, e["tb"].at(s + 1))
            for b in range(QW):
                n = QW * s + b
                pe.wait_ge(e["acc"].sem, e["acc"].at(n - 1))
                pe.wait_ge(e["sc"].sem, e["sc"].at(n - 1))
                for c in (2, 0, 3, 1):
                    pe.matmul(bank(b % 2, c), tb[:, p, b, :],
                              w_e[:, 4 * c:4 * c + 4, :].rearrange("p e n -> p (e n)"),
                              start=True, stop=True).then_inc(e["y"].sem, 1)

        def moe_act_step(act, s, p, runs):
            if runs(1):
                act.wait_ge(e["ld"].sem, e["ld"].at(s + 2))
                act.activation(le[:], le[:], ACT.Exp).then_inc(e["ex"].sem, 1)
            if runs(0):
                act.wait_ge(e["gate"].sem, e["gate"].at(s + 1))
                for b in range(QW):
                    n = QW * s + b
                    act.wait_ge(e["p1"].sem, e["p1"].at(n - 1))
                    for x in range(NA):
                        ex = E - NA + x
                        if x % 4 == 0:
                            act.wait_ge(e["y"].sem, e["y"].at(4 * n + (1 if x == 0 else 3)))
                        ins = act.activation(sc[:, b % 2, x, :],
                                             bank(b % 2, ex // 4)[:, ex % 4 * D:(ex % 4 + 1) * D],
                                             ACT.Copy, scale=gate[:, p, b, ex:ex + 1])
                    ins.then_inc(e["sc"].sem, 1)

        def moe_pool_step(po, s, p, runs):
            q = 1 - p
            if runs(1):
                po.wait_ge(e["y"].sem, e["y"].at(4 * QW * s))
                apart(po)
                po.tensor_copy(tb[:, q], T[:, bass.ds(QW * (s + 1), QW), :]).then_inc(e["tb"].sem, 1)
            if runs(0):
                for b in range(QW):
                    n, b2 = QW * s + b, b % 2
                    po.wait_ge(e["sc"].sem, e["sc"].at(n + 1))
                    po.wait_ge(e["p3"].sem, e["p3"].at(n - 1))
                    po.tensor_tensor(padd[:, b2], sc[:, b2, 0:4], sc[:, b2, 4:8], ALU.add).then_inc(e["p1"].sem, 1)
                    po.wait_ge(e["p1"].sem, e["p1"].at(n + 1))
                    po.tensor_tensor(padd[:, b2, 0:2], padd[:, b2, 0:2], padd[:, b2, 2:4], ALU.add
                                     ).then_inc(e["p2"].sem, 1)
                    po.wait_ge(e["p2"].sem, e["p2"].at(n + 1))
                    po.wait_ge(e["out"].sem, e["out"].at(n - 1))
                    po.tensor_tensor(psum3[:, b2], padd[:, b2, 0], padd[:, b2, 1], ALU.add).then_inc(e["p3"].sem, 1)

        def moe_output(v, s, p, b):
            n, b2 = QW * s + b, b % 2
            v.wait_ge(e["acc"].sem, e["acc"].at(n + 1))
            v.scalar_tensor_tensor(acc[:, b2, 0, :], acc[:, b2, 0, :], epsT[:, p, b:b + 1], acc[:, b2, 1, :],
                                   ALU.add, ALU.add).then_inc(e["ab"].sem, 1)
            v.wait_ge(e["ab"].sem, e["ab"].at(n + 1))
            v.wait_ge(e["p3"].sem, e["p3"].at(n + 1))
            if not (isinstance(s, int) and n < 2):
                v.wait_ge(e_st[b2], 8 * (n - b2))
            v.tensor_tensor(ob[:, b2, :], acc[:, b2, 0, :], psum3[:, b2], ALU.add).then_inc(e["out"].sem, 1)

        def moe_dve_step(v, s, p, runs):
            if runs(1):
                moe_logits(v, s + 1)
            if not runs(0):
                for n in range(NGATE):
                    gate_stage(v, n, s + 1, 1 - p)
                return
            v.wait_ge(e["gate"].sem, e["gate"].at(s + 1))
            for b in range(QW):
                n, b2 = QW * s + b, b % 2
                v.wait_ge(e["out"].sem, e["out"].at(n - 1))
                for x in range(ND):
                    src = bank(b2, x // 4)[:, x % 4 * D:(x % 4 + 1) * D]
                    total = acc[:, b2, x % 2, :]
                    if x % 4 == 0:
                        v.wait_ge(e["y"].sem, e["y"].at(4 * n + (2 if x == 0 else 4)))
                    if x >= 2:
                        v.wait_ge(e["gp"].sem, e["gp"].at((ND - 1) * n + x - 1))
                    if x == 1:
                        ins = v.tensor_scalar(total, src, gate[:, p, b, x:x + 1], None, ALU.mult)
                    else:
                        ins = v.scalar_tensor_tensor(total, src, gate[:, p, b, x:x + 1],
                                                     X[:, n, :] if x == 0 else total, ALU.mult, ALU.add)
                    ins.then_inc((e["gp"] if x < ND - 1 else e["acc"]).sem, 1)
                    if runs(1) and 1 <= x <= 6 and 6 * b + x - 1 < NGATE:
                        gate_stage(v, 6 * b + x - 1, s + 1, 1 - p)
                    if x == 4 and b > 0:
                        moe_output(v, s, p, b - 1)
                    elif x == 4 and not (isinstance(s, int) and s == 0):
                        moe_output(v, s - 1, 1 - p, QW - 1)

        def moe_store(sp):
            with sp.Fori(0, B // 2) as t:
                for b2 in range(2):
                    sp.wait_ge(e["out"].sem, e["out"].at(2 * t + b2 + 1))
                    sp.dma_start(out[bass.ds(2 * t + b2, 1)].rearrange("o t d -> (o t) d"),
                                 ob[:, b2, :]).then_inc(e_st[b2], 16)
            for b2 in range(2):
                sp.wait_ge(e_st[b2], 16 * (B // 2))

        @block.vector
        def _(v):
            v.memset(QK[:].rearrange("p a t h r -> p (a t h r)").bitcast(F32), 0.0)
            v.memset(V[:], 0.0).then_inc(s_init, 1)
            v.wait_ge(s_init, 1)
            v.memset(V[:, :, :, DH:DH + 1], 1.0)
            v.memset(negm[:], 0.0)
            v.memset(mean[:], 1.0 / 128)
            v.memset(neghalf[:], -0.5)
            v.memset(p18[:], -1.0)
            v.wait_ge(s_c, 16 * 6)
            v.tensor_copy(id16[:], id32[:])
            v.tensor_copy(idb[:], id32[:])
            v.tensor_copy(sel[:], sel32[:].unsqueeze(2).broadcast_to([128, H, 128])).then_inc(s_init, 1)
            v.wait_ge(s_wt, 1)
            v.tensor_copy(w_dT[:, 0, :], B0[0:DL, 0:128])
            v.tensor_copy(w_dT[:, 1, :], B0[0:DL, 128:256]).then_inc(s_wtc, 1)
            v.wait_ge(s_wf, 1)
            v.tensor_copy(w_mla[:, MQ:MK], B2[:, 0:128])
            v.tensor_copy(w_mla[:, MR:MR + H * DR], B2[:, 128:128 + H * DR])
            v.tensor_copy(w_mla[:, MK:MR], B3[:, 0:256]).then_inc(s_prep, 1)
            v.wait_ge(s_prep, 1)
            v.wait_ge(s_x0, 16)
            seam(v, dve_step, MLA)
            v.wait_ge(s_x1, 16 * 3)
            steady(v, dve_step, MLA)
            v.wait_ge(s_w2, 16 * NW2)
            for x, w in ((0, w_x1), (2, w_x2)):
                v.tensor_copy(w[:].rearrange("p a (h d) -> p a h d", d=DH),
                              w_raw[:, x:x + 2, :].rearrange("p a (d h) -> p a h d", d=DH))
            v.wait_ge(s_m, 32)
            v.tensor_copy(mask_f[:], mask_b[:]).then_inc(s_init, 1)
            v.wait_ge(s_small, 1)
            v.tensor_copy(w_r[:], B0[:, 256:256 + E])
            v.tensor_scalar(keep[:], B0[0:SC, 320:320 + B], -1.0, 1.0, ALU.mult, ALU.add)
            v.tensor_scalar(maskbias[:], B0[0:SC, 320:320 + B], MASKED * SCALE_X, None, ALU.mult
                            ).then_inc(s_prep2, 1)
            for k in (SA, CA):
                seam(v, dve_step, k)
                if k == SA:
                    v.wait_ge(sems[MLA]["took"].sem, sems[MLA]["took"].at(B))
                steady(v, dve_step, k)
            seam(v, dve_step, CA + 1)
            v.wait_ge(sems[CA]["done"].sem, sems[CA]["done"].at(B))
            pipeline(v, mlp_dve_step, 2, 3)
            v.wait_ge(f["l"].sem, f["l"].at(NQ))
            pipeline(v, moe_dve_step, 1, 0)
            moe_output(v, NQ - 1, (NQ - 1) % 2, QW - 1)

        def warm_up(pe, k):
            pe.wait_ge(sems[k]["v"].sem, sems[k]["v"].at(3))
            for _ in range(3):
                pe.matmul(B0[:, 0:MEND], id32[:], w_mla[:], start=True, stop=True)

        @block.tensor
        def _(pe):
            pe.wait_ge(s_c, 16 * 6)
            pe.wait_ge(s_w, 16 * 8)
            pe.transpose(B0[0:DL, 0:128], w_dqkv[:, 0:DL], id32[:])
            pe.transpose(B0[0:DL, 128:256], w_dqkv[:, DL:2 * DL], id32[:]).then_inc(s_wt, 1)
            pe.wait_ge(s_wtc, 1)
            pe.matmul(B2[:, 0:192], w_dT[:, 0, :], w_uq[:], start=True, stop=True)
            pe.matmul(B3[:, 0:256], w_dT[:, 1, :], w_ukv[:], start=True, stop=True).then_inc(s_wf, 1)
            pe.wait_ge(s_prep, 1)
            seam(pe, pe_step, MLA)
            warm_up(pe, MLA)
            steady(pe, pe_step, MLA)
            pe.wait_ge(s_init, 3)
            pe.wait_ge(sems[MLA]["v"].sem, sems[MLA]["v"].at(B - 1))
            pe.transpose(B0[0:SC, 320:320 + B], mask_f[:], id32[0:B, 0:B])
            pe.transpose(B0[:, 256:256 + E], w_rt[:], id32[0:E, 0:E]).then_inc(s_small, 1)
            pe.wait_ge(s_prep2, 1)
            for k in (SA, CA):
                seam(pe, pe_step, k)
                warm_up(pe, k)
                steady(pe, pe_step, k)
            seam(pe, pe_step, CA + 1)
            pe.wait_ge(sems[CA]["done"].sem, sems[CA]["done"].at(B))
            pipeline(pe, mlp_pe_step, 2, 3)
            pe.wait_ge(f["l"].sem, f["l"].at(NQ))
            pipeline(pe, moe_pe_step, 1, 0)

        @block.scalar
        def _(act):
            act.wait_ge(s_prep, 1)
            seam(act, act_step, MLA)
            steady(act, act_step, MLA)
            act.wait_ge(s_prep2, 1)
            for k in (SA, CA):
                seam(act, act_step, k)
                if k == SA:
                    act.activation(mask_terms[:].rearrange("p b t -> p (b t)"),
                                   mask_rows[:].rearrange("p b t -> p (b t)"),
                                   ACT.Copy, scale=MASKED).then_inc(s_mr, 1)
                steady(act, act_step, k)
            seam(act, act_step, CA + 1)
            act.wait_ge(sems[CA]["done"].sem, sems[CA]["done"].at(B))
            pipeline(act, mlp_act_step, 2, 3)
            act.wait_ge(f["l"].sem, f["l"].at(NQ))
            pipeline(act, moe_act_step, 1, 0)

        @block.gpsimd
        def _(po):
            for signal in (*attn_sem.values(), *(x.sem for x in f.values()), *(x.sem for x in e.values())):
                po.sem_inc(signal, LEAD)
            po.wait_ge(s_prep, 1)
            seam(po, pool_step, MLA)
            steady(po, pool_step, MLA)
            for k in (SA, CA):
                seam(po, pool_step, k)
                steady(po, pool_step, k)
                if k == SA:
                    po.wait_ge(s_mr, 1)
            seam(po, pool_step, CA + 1)
            po.wait_ge(sems[CA]["done"].sem, sems[CA]["done"].at(B))
            pipeline(po, mlp_pool_step, 2, 3)
            po.wait_ge(f["l"].sem, f["l"].at(NQ))
            pipeline(po, moe_pool_step, 1, 0)

        @block.sync
        def _(sp):
            xv = a["x"].rearrange("b t d -> t b d")
            sp.dma_start(X[:, 0:4, :], xv[:, 0:4, :]).then_inc(s_x0, 16)
            for dst, name in ((id32[:], "c_ident"), (cosT[:], "c_cos"), (nsin[:], "c_nsin"),
                              (psin[:], "c_psin"), (causal[:], "c_causal"), (sel32[:], "c_sel")):
                sp.dma_start(dst, a[name]).then_inc(s_c, 16)
            sp.dma_start(w_dqkv[:, 0:DL], a["L0_attn_W_DQ"]).then_inc(s_w, 16)
            sp.dma_start(w_dqkv[:, DL:2 * DL], a["L0_attn_W_DKV"]).then_inc(s_w, 16)
            sp.dma_start(w_uq[:, 0:H * DH], a["L0_attn_W_UQ"]).then_inc(s_w, 16)
            sp.dma_start(w_uq[:, H * DH:], a["L0_attn_W_QR"]).then_inc(s_w, 16)
            sp.dma_start(w_ukv[:, 0:H * DH], a["L0_attn_W_UK"]).then_inc(s_w, 16)
            sp.dma_start(w_ukv[:, H * DH:], a["L0_attn_W_UV"]).then_inc(s_w, 16)
            sp.dma_start(w_mla[:, MEND - DR:MEND], a["L0_attn_W_KR"]).then_inc(s_w, 16)
            sp.dma_start(w_o[:, 0, :], a["L0_attn_W_O"]).then_inc(s_w, 16)
            for b0 in range(4, B, 20):
                sp.dma_start(X[:, b0:b0 + 20, :], xv[:, b0:b0 + 20, :]).then_inc(s_x1, 16)
            for k, name in enumerate(("q1W", "w1W", "q2W", "w2W")):
                sp.dma_start(w_raw[:, k, :], a["L0_xattn_" + name]).then_inc(s_w2, 16)
            sp.dma_start(w_o[:, 1, :], a["L0_xattn_o1W"]).then_inc(s_w2, 16)
            sp.dma_start(w_o[:, 2, :], a["L0_xattn_o2W"]).then_inc(s_w2, 16)
            sp.dma_start(w_f1[:], a["L0_xattn_ffW1"]).then_inc(s_w2, 16)
            sp.dma_start(w_f2[:], a["L0_xattn_ffW2"].rearrange("(c p) n -> p c n", p=128)).then_inc(s_w2, 16)
            sp.dma_start(b_f1[:], a["L0_xattn_ffb1"].rearrange("(c p) -> p c", p=128),
                         allow_slow_non_contiguous=True).then_inc(s_w2, 16)
            sp.dma_start(b_f2[:], a["L0_xattn_ffb2"].rearrange("(p o) -> p o", o=1)).then_inc(s_w2, 16)
            for k, name in enumerate(("g1", "b1", "g2", "b2", "g3", "b3")):
                sp.dma_start(gb[:, k, :], a["L0_xattn_" + name].partition_broadcast(128)).then_inc(s_w2, 16)
            sp.dma_start(w_rt[:], a["L0_ffn_router_w"]).then_inc(s_w2, 16)
            sp.dma_start(b_r[:], a["L0_ffn_router_b"].partition_broadcast(128)).then_inc(s_w2, 16)
            sp.dma_start(w_e[:], a["L0_ffn_expert_w"].rearrange("e h n -> h e n")).then_inc(s_w2, 16)
            sp.dma_start(mask_rows[:], a["mask_Bx1xS2x1_bk0"].rearrange("b o s p -> (b o) (s p)")
                         .partition_broadcast(128)).then_inc(s_m, 16)
            sp.dma_start(mask_b[:], a["mask_Bx1xS2x1_bk0"].rearrange("b o s p -> b (o s p)")).then_inc(s_m, 16)

            s = sems[CA]

            for i in range(2):
                sp.dma_start(cx[:, i, :], a["ctx_1024"][i]).then_inc(s_ctx[i], 16)
            with sp.Fori(1, B // 2) as t:
                for p in range(2):
                    sp.wait_ge(s["xnT_ps"].sem, s["xnT_ps"].at(2 * t + p - 1))
                    sp.dma_start(cx[:, p, :],
                                 a["ctx_1024"][bass.ds(2 * t + p, 1)].rearrange("o s d -> (o s) d")
                                 ).then_inc(s_ctx[p], 16)
            moe_store(sp)


_INS = ["x", "ctx_1024", "mask_Bx1xS2x1_bk0", "L0_attn_W_DQ", "L0_attn_W_UQ", "L0_attn_W_QR", "L0_attn_W_DKV",
        "L0_attn_W_UK", "L0_attn_W_UV", "L0_attn_W_KR", "L0_attn_W_O", "L0_xattn_q1W", "L0_xattn_w1W",
        "L0_xattn_o1W", "L0_xattn_q2W", "L0_xattn_w2W", "L0_xattn_o2W", "L0_xattn_ffW1", "L0_xattn_ffb1",
        "L0_xattn_ffW2", "L0_xattn_ffb2", "L0_xattn_g1", "L0_xattn_b1", "L0_xattn_g2", "L0_xattn_b2",
        "L0_xattn_g3", "L0_xattn_b3", "L0_ffn_router_w", "L0_ffn_router_b", "L0_ffn_expert_w"]


def shape_constants():
    f32 = np.float32
    ang = np.arange(S, dtype=f32)[:, None] * (f32(10000.0) ** (-np.arange(0, DR, 2, dtype=f32) / f32(DR)))
    ang = ang.astype(f32)
    key, query = np.arange(S)[:, None], np.arange(S)[None, :]
    part = np.arange(128)
    return {
        "c_ident": np.eye(128, dtype=f32),
        "c_cos": np.repeat(np.cos(ang), 2, axis=1).astype(f32),
        "c_nsin": (-np.sin(ang)).astype(f32),
        "c_psin": np.sin(ang).astype(f32),
        "c_causal": np.where(query >= key, math.exp(CLIP * SCALE_MLA), 0.0).astype(f32),
        "c_sel": (part[:, None] == np.array([32 * (h % NJ) + h // NJ for h in range(H)])[None, :]).astype(f32),
    }


def kernel(**inputs):
    import concourse.bacc as _bacc
    from concourse.bass_utils import run_bass_kernel_spmd as _run

    nc = _bacc.Bacc("TRN2", target_bir_lowering=False, num_devices=1)
    arrays, args = {}, {}
    given = {n: np.ascontiguousarray(inputs[n]) for n in _INS}
    for name, arr in {**given, **shape_constants()}.items():
        arrays[f"in_{name}"] = arr
        args[name] = nc.dram_tensor(f"in_{name}", arr.shape, mybir.dt.from_np(arr.dtype), kind="ExternalInput").ap()
    out = nc.dram_tensor("out_0_dram", (B, S, D), F32, kind="ExternalOutput").ap()
    decoder_kernel(nc, args, out)
    r = _run(nc, [arrays], core_ids=[0])
    return r.results[0]["out_0_dram"]
```
